# Optimizing a Trainium2 kernel written in Bass

```python
import numpy as np
import jax
import jax.numpy as jnp

def _softmax(x, axis=-1):
    return jax.nn.softmax(x, axis=axis)

def _gelu(x):
    return jax.nn.gelu(x, approximate=True)

def _silu(x):
    return jax.nn.silu(x)

def _sigmoid(x):
    return jax.nn.sigmoid(x)

def _layernorm(x, axis=-1, eps=1e-05):
    m = jnp.mean(x, axis=axis, keepdims=True)
    v = jnp.var(x, axis=axis, keepdims=True)
    return (x - m) / jnp.sqrt(v + eps)

def _scatter_add(tgt, idx, src, axis=0):
    return tgt.at[idx].add(src)

def _segment_sum(src, seg, n):
    return jax.ops.segment_sum(src, seg, n)
kernel_name = 'mk_seq_preln_d1_jaxref_r8_4159b4'

def setup_inputs(seed: int=0):
    np.random.seed(seed)
    _w = jnp.asarray

    def _L0_attn_setup():
        import jax, jax.numpy as jnp
        import numpy as np
        EPS = 1e-05
        CHUNK = 128

        def lightning_attn(q, k, v, ld, chunk=CHUNK):
            b, n, h, d = q.shape
            nc = n // chunk
            idx = jnp.arange(chunk)
            diff = idx[:, None] - idx[None, :]
            mask = diff >= 0
            D = jnp.exp(ld[:, None, None] * jnp.where(mask, diff, 0)) * mask
            q_decay = jnp.exp(ld[None, :] * (idx + 1)[:, None])
            k_decay = jnp.exp(ld[None, :] * (chunk - 1 - idx)[:, None])
            chunk_decay = jnp.exp(ld * chunk)
            qc = jnp.moveaxis(q.reshape(b, nc, chunk, h, d), 1, 0)
            kc = jnp.moveaxis(k.reshape(b, nc, chunk, h, d), 1, 0)
            vc = jnp.moveaxis(v.reshape(b, nc, chunk, h, d), 1, 0)

            def step(S, inp):
                qb, kb, vb = inp
                scores = jnp.einsum('bchd,bshd->bhcs', qb, kb) * D[None]
                o_intra = jnp.einsum('bhcs,bshd->bchd', scores, vb)
                o_inter = jnp.einsum('bchd,bhde->bche', qb, S) * q_decay[None, :, :, None]
                S_new = chunk_decay[None, :, None, None] * S + jnp.einsum('bshd,bshe->bhde', kb * k_decay[None, :, :, None], vb)
                return (S_new, o_intra + o_inter)
            S0 = jnp.zeros((b, h, d, d), dtype=q.dtype)
            S_final, oc = jax.lax.scan(step, S0, (qc, kc, vc))
            out = jnp.moveaxis(oc, 0, 1).reshape(b, n, h, d)
            return (out, S_final)

        def group_rmsnorm_fused_gate(o, gate, w, num_heads):
            b, n, d = o.shape
            hd = d // num_heads
            o = o * jax.nn.sigmoid(gate)
            og = o.reshape(b, n, num_heads, hd)
            og = og * jax.lax.rsqrt(jnp.mean(og * og, axis=-1, keepdims=True) + EPS)
            return og.reshape(b, n, d) * w
        key = jax.random.key(seed)
        ks = jax.random.split(key, 10)
        B, N, D, H = (2, 512, 256, 16)
        HD = D // H
        s = 1.0 / np.sqrt(D)
        x = jax.random.normal(ks[0], (B, N, D), dtype=jnp.float32)
        log_decay = -jax.random.uniform(ks[1], (H,), dtype=jnp.float32, minval=0.01, maxval=1.0)
        Wq = jax.random.normal(ks[2], (D, D), dtype=jnp.float32) * s
        Wk = jax.random.normal(ks[3], (D, D), dtype=jnp.float32) * s
        Wv = jax.random.normal(ks[4], (D, D), dtype=jnp.float32) * s
        Wo = jax.random.normal(ks[5], (D, D), dtype=jnp.float32) * s
        Wg1 = jax.random.normal(ks[6], (D, HD), dtype=jnp.float32) * s
        Wg2 = jax.random.normal(ks[7], (HD, D), dtype=jnp.float32) / np.sqrt(HD)
        norm_w = jnp.ones((D,), dtype=jnp.float32)
        return {'x': x, 'log_decay': log_decay, 'Wq': Wq, 'Wk': Wk, 'Wv': Wv, 'Wo': Wo, 'Wg1': Wg1, 'Wg2': Wg2, 'norm_w': norm_w}
    _L0_attn_in = _L0_attn_setup()

    def _L0_ffn_setup():
        import jax, jax.numpy as jnp
        import numpy as np
        H, I, E = (256, 512, 8)
        B, S = (2, 256)
        key = jax.random.key(seed)
        ks = jax.random.split(key, 5)
        scale = 0.02
        return {'hidden_states': jax.random.normal(ks[0], (B, S, H), dtype=jnp.float32), 'router_w': jax.random.normal(ks[1], (H, E), dtype=jnp.float32) * scale, 'gate_w': jax.random.normal(ks[2], (E, H, I), dtype=jnp.float32) * scale, 'up_w': jax.random.normal(ks[3], (E, H, I), dtype=jnp.float32) * scale, 'down_w': jax.random.normal(ks[4], (E, I, H), dtype=jnp.float32) * scale}
    _L0_ffn_in = _L0_ffn_setup()
    _d = {'L0_attn_x': _L0_attn_in['x'], 'L0_attn_log_decay': _L0_attn_in['log_decay'], 'L0_attn_Wq': _L0_attn_in['Wq'], 'L0_attn_Wk': _L0_attn_in['Wk'], 'L0_attn_Wv': _L0_attn_in['Wv'], 'L0_attn_Wo': _L0_attn_in['Wo'], 'L0_attn_Wg1': _L0_attn_in['Wg1'], 'L0_attn_Wg2': _L0_attn_in['Wg2'], 'L0_attn_norm_w': _L0_attn_in['norm_w'], 'L0_ffn_router_w': _L0_ffn_in['router_w'], 'L0_ffn_gate_w': _L0_ffn_in['gate_w'], 'L0_ffn_up_w': _L0_ffn_in['up_w'], 'L0_ffn_down_w': _L0_ffn_in['down_w']}
    _x0 = _d['L0_attn_x']
    _d['L0_attn_x'] = jax.random.normal(jax.random.fold_in(jax.random.key(seed), 1), (8, 256, 256), dtype=_x0.dtype)
    del _x0
    return _d

def reference(L0_attn_x, L0_attn_log_decay, L0_attn_Wq, L0_attn_Wk, L0_attn_Wv, L0_attn_Wo, L0_attn_Wg1, L0_attn_Wg2, L0_attn_norm_w, L0_ffn_router_w, L0_ffn_gate_w, L0_ffn_up_w, L0_ffn_down_w):

    def _L0_attn_ref(x, log_decay, Wq, Wk, Wv, Wo, Wg1, Wg2, norm_w):
        import jax, jax.numpy as jnp
        import numpy as np
        EPS = 1e-05
        CHUNK = 128

        def lightning_attn(q, k, v, ld, chunk=CHUNK):
            b, n, h, d = q.shape
            nc = n // chunk
            idx = jnp.arange(chunk)
            diff = idx[:, None] - idx[None, :]
            mask = diff >= 0
            D = jnp.exp(ld[:, None, None] * jnp.where(mask, diff, 0)) * mask
            q_decay = jnp.exp(ld[None, :] * (idx + 1)[:, None])
            k_decay = jnp.exp(ld[None, :] * (chunk - 1 - idx)[:, None])
            chunk_decay = jnp.exp(ld * chunk)
            qc = jnp.moveaxis(q.reshape(b, nc, chunk, h, d), 1, 0)
            kc = jnp.moveaxis(k.reshape(b, nc, chunk, h, d), 1, 0)
            vc = jnp.moveaxis(v.reshape(b, nc, chunk, h, d), 1, 0)

            def step(S, inp):
                qb, kb, vb = inp
                scores = jnp.einsum('bchd,bshd->bhcs', qb, kb) * D[None]
                o_intra = jnp.einsum('bhcs,bshd->bchd', scores, vb)
                o_inter = jnp.einsum('bchd,bhde->bche', qb, S) * q_decay[None, :, :, None]
                S_new = chunk_decay[None, :, None, None] * S + jnp.einsum('bshd,bshe->bhde', kb * k_decay[None, :, :, None], vb)
                return (S_new, o_intra + o_inter)
            S0 = jnp.zeros((b, h, d, d), dtype=q.dtype)
            S_final, oc = jax.lax.scan(step, S0, (qc, kc, vc))
            out = jnp.moveaxis(oc, 0, 1).reshape(b, n, h, d)
            return (out, S_final)

        def group_rmsnorm_fused_gate(o, gate, w, num_heads):
            b, n, d = o.shape
            hd = d // num_heads
            o = o * jax.nn.sigmoid(gate)
            og = o.reshape(b, n, num_heads, hd)
            og = og * jax.lax.rsqrt(jnp.mean(og * og, axis=-1, keepdims=True) + EPS)
            return og.reshape(b, n, d) * w
        b, n, d = x.shape
        H = log_decay.shape[0]
        hd = d // H
        q = jax.nn.silu(jnp.einsum('bnd,de->bne', x, Wq).reshape(b, n, H, hd))
        k = jax.nn.silu(jnp.einsum('bnd,de->bne', x, Wk).reshape(b, n, H, hd))
        v = jax.nn.silu(jnp.einsum('bnd,de->bne', x, Wv).reshape(b, n, H, hd))
        o, _ = lightning_attn(q, k, v, log_decay)
        o = o.reshape(b, n, d)
        gate = jnp.einsum('bnk,kd->bnd', jnp.einsum('bnd,dk->bnk', x, Wg1), Wg2)
        o = group_rmsnorm_fused_gate(o, gate, norm_w, H)
        return jnp.einsum('bnd,de->bne', o, Wo)

    def _L0_ffn_ref(hidden_states, router_w, gate_w, up_w, down_w):
        import jax, jax.numpy as jnp
        import numpy as np
        H, I, E = (256, 512, 8)
        B, S = (2, 256)
        hidden_shape = hidden_states.shape
        x = hidden_states.reshape(-1, hidden_shape[-1])
        route = jax.nn.sigmoid(x @ router_w)
        max_ind = jnp.argmax(route, axis=1)
        max_prob = jnp.take_along_axis(route, max_ind[:, None], axis=1)
        out = jnp.zeros_like(x)
        num_experts = gate_w.shape[0]
        for e in range(num_experts):
            mask = (max_ind == e)[:, None]
            h = jax.nn.silu(x @ gate_w[e]) * (x @ up_w[e])
            out = out + jnp.where(mask, h @ down_w[e], 0.0)
        out = out * max_prob
        return out.reshape(hidden_shape)
    x = L0_attn_x
    x = x + _L0_attn_ref(_layernorm(x, axis=-1), L0_attn_log_decay, L0_attn_Wq, L0_attn_Wk, L0_attn_Wv, L0_attn_Wo, L0_attn_Wg1, L0_attn_Wg2, L0_attn_norm_w)
    x = x + _L0_ffn_ref(_layernorm(x, axis=-1), L0_ffn_router_w, L0_ffn_gate_w, L0_ffn_up_w, L0_ffn_down_w)
    return x

_drawn_inputs = setup_inputs


def setup_inputs(seed=0):
    import zlib

    import numpy as np

    out = dict(_drawn_inputs(seed))
    spreads = {'L0_attn_norm_w': (1.0, 0.2)}
    factors = {'L0_ffn_router_w': 5.933,
     'L0_ffn_gate_w': 5.696,
     'L0_ffn_up_w': 5.651,
     'L0_ffn_down_w': 5.627}
    for name, (base, spread) in spreads.items():
        noise = np.random.default_rng([zlib.crc32(name.encode()), seed]).standard_normal(out[name].shape)
        drawn = base * np.exp(spread * noise) if base else spread * noise
        out[name] = jnp.asarray(drawn.astype(out[name].dtype))
    for name, factor in factors.items():
        out[name] = (out[name] * factor).astype(out[name].dtype)
    return out
```

```python
from contextlib import ExitStack

import concourse.bass as bass
from concourse import mybir

ALU = mybir.AluOpType
ACT = mybir.ActivationFunctionType
AX = mybir.AxisListType
F32 = mybir.dt.float32
BF16 = mybir.dt.bfloat16
I32 = mybir.dt.int32
U32 = mybir.dt.uint32

P = 128
EPS = 1e-5


class Tile:

    def __init__(self, pair, half):
        self.pair, self.half = pair, half

    def index(self):
        return self.pair * 2 + self.half

    def later(self, n):
        return Tile(self.pair + (self.half + n) // 2, (self.half + n) % 2)

    def known(self):
        return isinstance(self.pair, int)


def lightning_block(nc, x, log_decay, wq, wk, wv, wo, wg1, wg2, norm_w, router_w, gate_w, up_w, down_w, out):
    B, N, D = x.shape
    H = log_decay.shape[0]
    HD = D // H
    E, _, F = gate_w.shape
    T = B * N // P
    KC = D // P
    FC = F // P
    HPC = P // HD
    SLOTS = T + E - 1
    ROOM = B * N + P
    ROWS = E * ROOM + P
    GU = 2 * KC * F
    EW = GU + FC * D
    REST = D + 2
    ROW = D + REST
    SKIP = 1 << 20
    assert N == 2 * P and D == 2 * P and F == 512 and H * HD == D and HD == 16

    x_rows = x.rearrange("b n d -> (b n) d")
    out_rows = out.rearrange("b n d -> (b n) d")
    sorted_rows = nc.dram_tensor("sorted_rows", (ROWS, ROW), F32, kind="Internal").ap()

    with ExitStack() as ctx:
        def sb(name, shape, dt=F32):
            return ctx.enter_context(nc.sbuf_tensor(name, shape, dt))

        def ps(name):
            return ctx.enter_context(nc.psum_tensor(name, [P, 512], F32))

        sems = {}

        def sem(name):
            if name not in sems:
                sems[name] = ctx.enter_context(nc.semaphore(name))
            return sems[name]

        w_exp = sb("w_exp", [P, E * EW])
        w_qkvg = sb("w_qkvg", [P, KC, 4 * D])
        w_o = sb("w_o", [P, KC, D])
        w_g1T = sb("w_g1T", [HD, D])
        w_g2 = sb("w_g2", [HD, D])
        w_r = sb("w_r", [P, KC, E])
        nw = sb("nw", [P, KC])
        ident = sb("ident", [P, P])
        upper = sb("upper", [P, P], BF16)
        ones_bf = sb("ones_bf", [P, P], BF16)
        same_head = sb("same_head", [P, P])
        neg_half = sb("neg_half", [P, H])
        parity = sb("parity", [P, 2])
        ld_row = sb("ld_row", [P, H])
        ld_exp = sb("ld_exp", [P, D])
        ld_col = sb("ld_col", [P, KC])
        dist = sb("dist", [P, P])
        ahead = sb("ahead", [P, P])
        behind = sb("behind", [P, 1])
        decay = sb("decay", [P, H, P])
        k_decay = sb("k_decay", [P, D])
        q_decay = sb("q_decay", [P, KC, P])
        desc = sb("desc", [P, E])
        base = sb("base", [P, E])
        pad_row = sb("pad_row", [P, ROW])
        xin = [sb(f"xin{i}", [P, D]) for i in range(2)]
        xn = [sb(f"xn{i}", [P, D]) for i in range(2)]
        xT = [sb(f"xT{i}", [P, KC, P]) for i in range(2)]
        st1 = [sb(f"st1{i}", [P, 6]) for i in range(2)]
        mv1 = [sb(f"mv1{i}", [P, 2]) for i in range(2)]
        ve1 = [sb(f"ve1{i}", [P, 1]) for i in range(2)]
        rs1 = [sb(f"rs1{i}", [P, 1]) for i in range(2)]
        qk = [sb(f"qk{i}", [P, 2 * D]) for i in range(2)]
        vx = [sb(f"vx{i}", [P, H // 2, 2, 2 * HD]) for i in range(2)]
        tg = [sb(f"tg{i}", [P, D]) for i in range(2)]
        qkT = [sb(f"qkT{i}", [P, 2 * KC, P]) for i in range(2)]
        q_blocks = [sb(f"q_blocks{i}", [P, KC, HPC, P]) for i in range(2)]
        kd = sb("kd", [P, D])
        qd = sb("qd", [P, KC, P])
        state = sb("state", [P, KC, P])
        probs = sb("probs", [P, H, P])
        og = [sb(f"og{i}", [P, D]) for i in range(2)]
        sq = [sb(f"sq{i}", [P, D]) for i in range(2)]
        oT = [sb(f"oT{i}", [P, KC, P]) for i in range(2)]
        hsum = [sb(f"hsum{i}", [P, H]) for i in range(2)]
        hmean = [sb(f"hmean{i}", [P, H]) for i in range(2)]
        hbits = [sb(f"hbits{i}", [P, H], U32) for i in range(2)]
        hguess = [sb(f"hguess{i}", [P, H], I32) for i in range(2)]
        hsq = [sb(f"hsq{i}", [P, H]) for i in range(2)]
        hstep = [sb(f"hstep{i}", [P, H]) for i in range(2)]
        hfirst = [sb(f"hfirst{i}", [P, H]) for i in range(2)]
        hpoly = [sb(f"hpoly{i}", [P, H]) for i in range(2)]
        hroot = [sb(f"hroot{i}", [P, H]) for i in range(2)]
        on = [sb(f"on{i}", [P, D]) for i in range(2)]
        onT = [sb(f"onT{i}", [P, KC, P]) for i in range(2)]
        st2 = [sb(f"st2{i}", [P, 6]) for i in range(2)]
        mv2 = [sb(f"mv2{i}", [P, 2]) for i in range(2)]
        ve2 = [sb(f"ve2{i}", [P, 1]) for i in range(2)]
        rs2 = [sb(f"rs2{i}", [P, 1]) for i in range(2)]
        pay = [sb(f"pay{i}", [P, ROW]) for i in range(2)]
        x2T = [sb(f"x2T{i}", [P, KC, P]) for i in range(2)]
        th = [sb(f"th{i}", [P, E]) for i in range(2)]
        route = [sb(f"route{i}", [P, E]) for i in range(2)]
        cand = [sb(f"cand{i}", [P, E]) for i in range(2)]
        cmax = [sb(f"cmax{i}", [P, 1]) for i in range(2)]
        mask = [sb(f"mask{i}", [P, E], BF16) for i in range(2)]
        seen = sb("seen", [P, E], BF16)
        rank = [sb(f"rank{i}", [P, E]) for i in range(2)]
        prod = [sb(f"prod{i}", [P, E]) for i in range(2)]
        posf = [sb(f"posf{i}", [P, 1]) for i in range(2)]
        pos = [sb(f"pos{i}", [P, 1], U32) for i in range(2)]
        tok = sb("tok", [P, 1], I32)
        cnt = sb("cnt", [1, E])
        steps = sb("steps", [1, E, T])
        over = sb("over", [1, E, T])
        need = sb("need", [1, E])
        zero_row = sb("zero_row", [1, E])
        last = sb("last", [1, E])
        first = sb("first", [1, E])
        slot_no = sb("slot_no", [1, SLOTS, E])
        t_ge = sb("t_ge", [1, SLOTS, E])
        t_in = sb("t_in", [1, SLOTS, E])
        t_own = sb("t_own", [1, SLOTS, E])
        t_row = sb("t_row", [1, SLOTS, E])
        t_row2 = sb("t_row2", [1, SLOTS, E])
        t_val = sb("t_val", [1, SLOTS, E])
        t_wt = sb("t_wt", [1, SLOTS, E])
        r_sum = sb("r_sum", [1, SLOTS])
        w_sum = sb("w_sum", [1, SLOTS])
        woff_e = sb("woff_e", [1, E])
        slot_row = sb("slot_row", [1, SLOTS], I32)
        slot_w = sb("slot_w", [1, SLOTS], I32)
        fill_f = sb("fill_f", [1, E])
        fill_row = sb("fill_row", [1, E], I32)
        xs = [sb(f"xs{i}", [P, D]) for i in range(2)]
        rest = [sb(f"rest{i}", [P, REST]) for i in range(2)]
        tok_u = [sb(f"tok_u{i}", [P, 1], U32) for i in range(2)]
        xsT = [sb(f"xsT{i}", [P, KC, P]) for i in range(2)]
        hT = [probs[:, FC * i:FC * (i + 1), :] for i in range(2)]
        sg = [probs[:, FC * (i + 2):FC * (i + 3), :].rearrange("p c t -> p (c t)") for i in range(2)]
        hh = [q_blocks[i][:, 0, 0:FC, :].rearrange("p c t -> p (c t)") for i in range(2)]
        yo = [sb(f"yo{i}", [P, D]) for i in range(2)]

        PJ0, PJ1, TR, XT, SC0, SC1, OT, M = [ps(n) for n in ("PJ0", "PJ1", "TR", "XT", "SC0", "SC1", "OT", "M")]
        SC = [SC0, SC1]

        def v_heads(buf, c):
            pairs = HPC // 2
            flat = buf[:, c * pairs:(c + 1) * pairs, :, :].rearrange("p j a b -> p j (a b)")
            both = flat.rearrange("p j (a b) -> p j b a", a=4)[:, :, :, 0:4:3]
            return both.rearrange("p j b a -> p j a b")

        block = ctx.enter_context(nc.Block())

        def ready(eng, name, tile, per=1, extra=0):
            eng.wait_ge(sem(name), tile.index() * per + per + extra)

        def settle(eng):
            eng.sem_inc(sem("waited"), 1)

        def landed(eng, name, tile, n=1):
            eng.wait_ge(sem(f"{name}{tile.half}"), tile.pair * 16 * n + 16 * n)

        def freed(eng, name, tile, back=2, per=1, at=None):
            n = (tile.index() - back) * per + (per if at is None else at)
            if isinstance(n, int) and n <= 0:
                return
            eng.wait_ge(sem(name), n)

        def run_steps(eng, step, lo, hi):
            n = lo
            while n < hi:
                if n == 4:
                    with eng.Fori(2, (T - 2) // 2) as pair:
                        for half in range(2):
                            step(Tile(pair, half), None)
                    n = T - 2
                else:
                    step(Tile(n // 2, n % 2), n)
                    n += 1

        def valid(tile, n, shift):
            return n is None or 0 <= n + shift < T

        def pipeline(eng, parts):
            def step(tile, n):
                for part, shift in parts:
                    if valid(tile, n, shift):
                        part(tile.later(shift))
            run_steps(eng, step, -2, T + 2)

        def expert_pipeline(eng, parts):
            def step(s, n):
                for part, shift in parts:
                    if n is None or 0 <= n + shift < SLOTS:
                        part(s.later(shift))
            for n in range(-1, 4):
                step(Tile(n // 2, n % 2), n)
            with eng.Fori(2, (SLOTS - 1) // 2) as pair:
                step(Tile(pair, 0), None)
                step(Tile(pair, 1), None)
            for n in (SLOTS - 1, SLOTS):
                step(Tile(n // 2, n % 2), n)

        @block.sync
        def _(sp):
            for i, w in enumerate((wq, wk)):
                sp.dma_start(w_qkvg[:, :, i * D:(i + 1) * D], w.rearrange("(c p) e -> p c e", p=P)).then_inc(sem("w_qk_in"), 16)

            def load_x(t):
                freed(sp, "ln1", t)
                sp.dma_start(xin[t.half][:, :], x_rows[bass.ds(t.index() * P, P), :]).then_inc(sem(f"x_in{t.half}"), 16)

            def load_residual(t):
                if not (t.known() and t.index() < 2):
                    sp.wait_ge(sem(f"sorted{t.half}"), t.pair * 16)
                sp.dma_start(pay[t.half][:, D:2 * D], x_rows[bass.ds(t.index() * P, P), :]).then_inc(sem(f"res_in{t.half}"), 16)

            def load_expert(t):
                e = bass.ds(t.pair, 1)
                if t.half == 0:
                    for i, w in enumerate((gate_w, up_w)):
                        sp.dma_start(w_exp[:, bass.ds(t.pair * EW + i * KC * F, KC * F)].rearrange("p (c f) -> p c f", c=KC),
                                     w[e, :, :].rearrange("a (c p) f -> p (a c) f", p=P)).then_inc(sem("w_exp"), 16)
                else:
                    sp.dma_start(w_exp[:, bass.ds(t.pair * EW + GU, FC * D)].rearrange("p (c d) -> p c d", c=FC),
                                 down_w[e, :, :].rearrange("a (c p) d -> p (a c) d", p=P)).then_inc(sem("w_exp"), 16)

            pipeline(sp, [(load_x, 2), (load_residual, -1), (load_expert, 0)])

            sp.wait_ge(sem("pad"), 2)
            sp.wait_ge(sem("fill_row"), 1)
            for e in range(E):
                r = nc.sync.value_load(fill_row[0:1, e:e + 1], min_val=0, max_val=E * ROOM - P)
                sp.dma_start(sorted_rows[bass.ds(r, P), :], pad_row[:, :]).then_inc(sem("filled"), 16)
            sp.wait_ge(sem("filled"), 16 * E)
            sp.wait_ge(sem("spare_filled"), 16)
            sp.wait_ge(sem("sorted0"), 16 * (T // 2))
            sp.wait_ge(sem("sorted1"), 16 * (T // 2))
            sp.wait_ge(sem("slot_row"), 1)

            def row_of(s):
                return nc.sync.value_load(slot_row[0:1, bass.ds(s.index(), 1)], min_val=0, max_val=E * ROOM)

            def load_xs(s):
                r = row_of(s)
                freed(sp, "xsT_ps", s)
                sp.dma_start(xs[s.half][:, :], sorted_rows[bass.ds(r, P), 0:D]).then_inc(sem(f"xs_in{s.half}"), 16)

            def load_rest(s):
                r = row_of(s)
                freed(sp, "yo", s)
                sp.dma_start(rest[s.half][:, :], sorted_rows[bass.ds(r, P), D:ROW]).then_inc(sem(f"rest_in{s.half}"), 16)

            expert_pipeline(sp, [(load_xs, 1), (load_rest, -1)])

        @block.gpsimd
        def _(pool):
            pool.dma_start(ld_row[:, :], log_decay.rearrange("(a h) -> a h", a=1).broadcast_to([P, H])).then_inc(sem("ld_in"), 16)
            nc.gpsimd.memset(ident[:], 0.0).then_inc(sem("zeroed"), 1)
            pool.wait_ge(sem("zeroed"), 1)
            nc.gpsimd.affine_select(out=ident[:], in_=ident[:], compare_op=ALU.not_equal, fill=1.0, base=0,
                                    pattern=[[-1, P]], channel_multiplier=1).then_inc(sem("ident"), 1)
            nc.gpsimd.memset(neg_half[:], -0.5).then_inc(sem("neg_half"), 1)
            nc.gpsimd.iota(dist[:], pattern=[[1, P]], base=0, channel_multiplier=-1,
                           allow_small_or_imprecise_dtypes=True).then_inc(sem("dist"), 1)
            nc.gpsimd.iota(ahead[:], pattern=[[1, P]], base=1, channel_multiplier=0,
                           allow_small_or_imprecise_dtypes=True).then_inc(sem("dist"), 1)
            nc.gpsimd.iota(behind[:], pattern=[[0, 1]], base=P - 1, channel_multiplier=-1,
                           allow_small_or_imprecise_dtypes=True).then_inc(sem("dist"), 1)
            pool.wait_ge(sem("dist"), 1)
            nc.gpsimd.tensor_scalar(dist[:], dist[:], 0.0, None, ALU.max).then_inc(sem("dist"), 1)
            for i in range(2):
                nc.gpsimd.memset(q_blocks[i][:], 0.0).then_inc(sem("q_zeroed"), 1)
                nc.gpsimd.memset(vx[i][:], 0.0).then_inc(sem("v_zeroed"), 1)
            nc.gpsimd.memset(same_head[:], 1.0).then_inc(sem("sh"), 1)
            blocks = same_head[:].rearrange("p (h d) -> p h d", d=HD)
            pool.wait_ge(sem("sh"), 1)
            nc.gpsimd.affine_select(out=blocks, in_=blocks, compare_op=ALU.is_ge, fill=0.0, base=0,
                                    pattern=[[-HD, HPC], [0, HD]], channel_multiplier=1).then_inc(sem("sh"), 1)
            pool.wait_ge(sem("sh"), 2)
            nc.gpsimd.affine_select(out=blocks, in_=blocks, compare_op=ALU.is_ge, fill=0.0, base=HD - 1,
                                    pattern=[[HD, HPC], [0, HD]], channel_multiplier=-1).then_inc(sem("sh"), 1)
            nc.gpsimd.memset(ones_bf[:], 1.0).then_inc(sem("ones"), 1)
            pool.wait_ge(sem("ones"), 1)
            nc.gpsimd.affine_select(out=upper[:], in_=ones_bf[:], compare_op=ALU.is_gt, fill=0.0, base=0,
                                    pattern=[[1, P]], channel_multiplier=-1).then_inc(sem("ones"), 1)
            nc.gpsimd.memset(seen[:], 0.0).then_inc(sem("ones"), 1)
            nc.gpsimd.iota(desc[:], pattern=[[-1, E]], base=E, channel_multiplier=0,
                           allow_small_or_imprecise_dtypes=True).then_inc(sem("ones"), 1)
            nc.gpsimd.iota(base[:], pattern=[[ROOM, E]], base=0, channel_multiplier=0,
                           allow_small_or_imprecise_dtypes=True).then_inc(sem("ones"), 1)
            nc.gpsimd.iota(tok[:], pattern=[[0, 1]], base=0, channel_multiplier=1).then_inc(sem("tok"), 1)
            nc.gpsimd.iota(steps[:], pattern=[[0, E], [P, T]], base=0, channel_multiplier=0,
                           allow_small_or_imprecise_dtypes=True).then_inc(sem("consts"), 1)
            nc.gpsimd.memset(zero_row[:], 0.0).then_inc(sem("consts"), 1)
            nc.gpsimd.iota(slot_no[:], pattern=[[1, SLOTS], [0, E]], base=0, channel_multiplier=0,
                           allow_small_or_imprecise_dtypes=True).then_inc(sem("consts"), 1)
            nc.gpsimd.iota(woff_e[:], pattern=[[EW, E]], base=0, channel_multiplier=0,
                           allow_small_or_imprecise_dtypes=True).then_inc(sem("consts"), 1)
            nc.gpsimd.memset(pad_row[:, 0:ROW - 1], 0.0).then_inc(sem("pad"), 1)
            nc.gpsimd.memset(pad_row[:, ROW - 1:ROW].bitcast(I32), SKIP).then_inc(sem("pad"), 1)
            def decays(t):
                if t.half == 0:
                    ready(pool, "qk_silu", t)
                    pool.wait_ge(sem("k_decay"), 1)
                    if not (t.known() and t.index() == 0):
                        pool.wait_ge(sem("state_ps"), t.pair)
                    nc.gpsimd.tensor_tensor(kd[:], qk[0][:, D:2 * D], k_decay[:], ALU.mult).then_inc(sem("kd"), 1)
                else:
                    ready(pool, "qkT", t)
                    pool.wait_ge(sem("q_decay"), KC)
                    if not (t.known() and t.index() == 1):
                        freed(pool, "pv", t, per=4)
                    nc.gpsimd.tensor_tensor(qd[:], qkT[1][:, 0:KC, :], q_decay[:], ALU.mult).then_inc(sem("qd"), 1)

            def inverse_root(t, dst, mid, src, scale, eps, name):
                nc.gpsimd.tensor_scalar(mid, src, scale, eps, ALU.mult, ALU.add).then_inc(sem(name + "_sum"), 1)
                ready(pool, name + "_sum", t)
                settle(pool)
                nc.gpsimd.tensor_tensor(dst, mid, neg_half[:, 0:dst.shape[1]], ALU.pow).then_inc(sem(name), 1)

            def ln1_root(t):
                ready(pool, "ln1_mv", t)
                freed(pool, "ln1", t)
                settle(pool)
                inverse_root(t, rs1[t.half][:], ve1[t.half][:], mv1[t.half][:, 1:2], 1.0, EPS, "ln1_rs")

            def ln2_root(t):
                ready(pool, "ln2_mv", t)
                freed(pool, "x2n", t)
                settle(pool)
                inverse_root(t, rs2[t.half][:], ve2[t.half][:], mv2[t.half][:, 1:2], 1.0, EPS, "ln2_rs")

            def sort(t):
                if t.known() and t.index() < 2:
                    pool.wait_ge(sem("tok"), 1)
                else:
                    pool.wait_ge(sem(f"sorted{t.half}"), t.pair * 16)
                    ready(pool, "tok", t)
                settle(pool)
                nc.gpsimd.tensor_copy(pay[t.half][:, ROW - 1:ROW].bitcast(I32), tok[:]).then_inc(sem("tok_in"), 1)
                ready(pool, "tok_in", t)
                settle(pool)
                nc.gpsimd.tensor_scalar(tok[:], tok[:], float(P), None, ALU.add).then_inc(sem("tok"), 1)
                ready(pool, "pos", t)
                settle(pool)
                pool.indirect_dma_start(out=sorted_rows, out_offset=bass.IndirectOffsetOnAxis(ap=pos[t.half][:, 0:1], axis=0),
                                        in_=pay[t.half][:, :], in_offset=None).then_inc(sem(f"sorted{t.half}"), 16)

            def more_constants(t):
                if not (t.known() and t.index() == 0):
                    return
                pool.wait_ge(sem("decay_exp"), H)
                nc.gpsimd.affine_select(out=decay[:], in_=decay[:], compare_op=ALU.is_ge, fill=0.0, base=0,
                                        pattern=[[0, H], [1, P]], channel_multiplier=-1).then_inc(sem("decay"), 1)
                pool.wait_ge(sem("pad"), 2)
                pool.dma_start(sorted_rows[E * ROOM:ROWS, :], pad_row[:, :]).then_inc(sem("spare_filled"), 16)

            pool.wait_ge(sem("neg_half"), 1)
            pipeline(pool, [(ln1_root, 2), (more_constants, 2), (decays, 1), (sort, -2), (ln2_root, -1)])

            def store(s):
                ready(pool, "yo", s)
                settle(pool)
                pool.indirect_dma_start(out=out_rows, out_offset=bass.IndirectOffsetOnAxis(ap=tok_u[s.half][:, 0:1], axis=0),
                                        in_=yo[s.half][:, :], in_offset=None, bounds_check=B * N - 1,
                                        oob_is_err=False).then_inc(sem(f"stored{s.half}"), 16)
            with pool.Fori(0, SLOTS // 2) as pair:
                store(Tile(pair, 0))
                store(Tile(pair, 1))
            store(Tile(SLOTS // 2, 0))
            pool.wait_ge(sem("stored0"), 16 * (SLOTS // 2 + 1))
            pool.wait_ge(sem("stored1"), 16 * (SLOTS // 2))

        @block.scalar
        def _(act):
            with nc.allow_non_contiguous_dma("4,096 numbers, once"):
                act.dma_start(w_g1T[:, :], wg1.rearrange("d k -> k d")).then_inc(sem("w_g12_in"), 16)
            act.dma_start(w_g2[:, :], wg2).then_inc(sem("w_g12_in"), 16)
            act.dma_start(w_qkvg[:, :, 2 * D:3 * D], wv.rearrange("(c p) e -> p c e", p=P)).then_inc(sem("w_v_in"), 16)
            act.dma_start(w_o[:, :, :], wo.rearrange("(c p) e -> p c e", p=P)).then_inc(sem("w_o_in"), 16)
            with nc.allow_non_contiguous_dma("256 numbers, once"):
                act.dma_start(nw[:, :], norm_w.rearrange("(c p) -> p c", p=P)).then_inc(sem("w_o_in"), 16)
            act.dma_start(w_r[:, :, :], router_w.rearrange("(c p) e -> p c e", p=P)).then_inc(sem("w_r_in"), 16)
            act.wait_ge(sem("ld_in"), 16)
            nc.scalar.activation(ld_exp[:].rearrange("p (h d) -> p h d", d=HD),
                                 ld_row[:].rearrange("p (h a) -> p h a", a=1).broadcast_to([P, H, HD]), ACT.Copy).then_inc(sem("ld_exp"), 1)
            act.wait_ge(sem("dist"), 4)
            for h in range(H):
                nc.scalar.activation(decay[:, h, :], dist[:], ACT.Exp, scale=ld_row[:, h:h + 1]).then_inc(sem("decay_exp"), 1)
            act.wait_ge(sem("ld_exp"), 1)
            nc.scalar.activation(k_decay[:], ld_exp[:], ACT.Exp, scale=behind[:, 0:1]).then_inc(sem("k_decay"), 1)
            act.wait_ge(sem("w_g_ps"), 1)
            nc.scalar.activation(w_qkvg[:, :, 3 * D:4 * D], M[:, :].rearrange("p (c e) -> p c e", c=KC), ACT.Copy).then_inc(sem("w_g"), 1)
            act.wait_ge(sem("ld_T"), KC)
            for c in range(KC):
                nc.scalar.activation(ld_col[:, c:c + 1], TR[:, c * P:c * P + 1], ACT.Copy).then_inc(sem("ld_col"), 1)
            act.wait_ge(sem("ld_col"), KC)
            for c in range(KC):
                nc.scalar.activation(q_decay[:, c, :], ahead[:], ACT.Exp, scale=ld_col[:, c:c + 1]).then_inc(sem("q_decay"), 1)

            def xT_out(t):
                ready(act, "xT_ps", t)
                freed(act, "vg_ps", t)
                nc.scalar.activation(xT[t.half][:].rearrange("p c t -> p (c t)"), XT[:, 0:D], ACT.Copy).then_inc(sem("xT"), 1)

            def oT_out(t):
                ready(act, "pv", t, 4)
                freed(act, "o_turned", t)
                nc.scalar.activation(oT[t.half][:].rearrange("p c t -> p (c t)"), OT[:, 0:D], ACT.Copy).then_inc(sem("oT"), 1)

            def onT_out(t):
                ready(act, "on_turned", t)
                freed(act, "attn_ps", t)
                nc.scalar.activation(onT[t.half][:].rearrange("p c t -> p (c t)"), XT[:, 0:D], ACT.Copy).then_inc(sem("onT"), 1)

            def qk_silu(t):
                ready(act, "qk_ps", t)
                freed(act, "qkT_ps", t)
                if t.half == 0:
                    if not (t.known() and t.index() == 0):
                        act.wait_ge(sem("kd"), t.pair)
                nc.scalar.activation(qk[t.half][:, :], PJ0[:, :], ACT.Silu).then_inc(sem("qk_silu"), 1)

            def v_silu(t):
                ready(act, "vg_ps", t)
                freed(act, "pv", t, per=4)
                if t.known() and t.index() < 2:
                    act.wait_ge(sem("v_zeroed"), 2)
                for c in range(KC):
                    nc.scalar.activation(v_heads(vx[t.half], c),
                                         PJ1[:, c * P:(c + 1) * P].rearrange("p (j a b) -> p j a b", a=2, b=HD),
                                         ACT.Silu).then_inc(sem("v"), 1)
                freed(act, "og", t)
                nc.scalar.activation(tg[t.half][:], PJ1[:, D:2 * D], ACT.Tanh,
                                     scale=0.5).then_inc(sem("tg"), 1)

            def qkT_out(t):
                ready(act, "qkT_ps", t)
                freed(act, "scored", t, per=4)
                if t.half == 1 and not (t.known() and t.index() == 1):
                    act.wait_ge(sem("qd"), t.pair)
                if t.known() and t.index() == 0:
                    act.wait_ge(sem("parity"), 2)
                if t.known() and t.index() < 2:
                    act.wait_ge(sem("q_zeroed"), 2)
                for j in range(HPC // 2):
                    r = slice(32 * j, 32 * j + 32)
                    for a in range(2):
                        nc.scalar.activation(q_blocks[t.half][r, :, 2 * j + a, :], TR[r, 0:D].rearrange("p (c t) -> p c t", c=KC),
                                             ACT.Copy, scale=parity[r, a:a + 1])
                lo = KC if t.half == 0 else 0
                nc.scalar.activation(qkT[t.half][:, lo:, :].rearrange("p c t -> p (c t)"), TR[:, lo * P:], ACT.Copy).then_inc(sem("qkT"), 1)

            def square(t):
                ready(act, "og", t)
                freed(act, "hsum", t)
                nc.scalar.activation(sq[t.half][:], og[t.half][:], ACT.Square).then_inc(sem("sq"), 1)

            def x2T_out(t):
                ready(act, "x2T_ps", t)
                freed(act, "logits_ps", t)
                nc.scalar.activation(x2T[t.half][:].rearrange("p c t -> p (c t)"), XT[:, D:2 * D], ACT.Copy).then_inc(sem("x2T"), 1)

            def logits_tanh(t):
                ready(act, "logits_ps", t)
                freed(act, "route", t)
                nc.scalar.activation(th[t.half][:], M[:, 0:E], ACT.Tanh, scale=0.5).then_inc(sem("th"), 1)

            pipeline(act, [(oT_out, -1), (xT_out, 1), (square, -1), (qk_silu, 1), (x2T_out, -2), (v_silu, 1),
                           (logits_tanh, -2), (qkT_out, 1), (onT_out, -1)])

            def xsT_out(s):
                ready(act, "xsT_ps", s)
                freed(act, "up_ps", s)
                nc.scalar.activation(xsT[s.half][:].rearrange("p c t -> p (c t)"), XT[:, 0:D], ACT.Copy).then_inc(sem("xsT"), 1)

            def h_silu(s):
                ready(act, "gate2_ps", s)
                freed(act, "hh", s)
                nc.scalar.activation(sg[s.half][:], SC0[:, :], ACT.Silu).then_inc(sem("sg"), 1)

            def hT_out(s):
                ready(act, "hT_ps", s)
                freed(act, "down_ps", s)
                nc.scalar.activation(hT[s.half][:].rearrange("p c t -> p (c t)"), TR[:, :], ACT.Copy).then_inc(sem("hT"), 1)

            expert_pipeline(act, [(hT_out, -1), (h_silu, 0), (xsT_out, 1)])

        @block.vector
        def _(dve):
            dve.wait_ge(sem("w_o_in"), 32)
            for c in range(KC):
                nc.vector.tensor_scalar(w_o[:, c, :], w_o[:, c, :], nw[:, c:c + 1], 3.0 / 8.0, ALU.mult, ALU.mult).then_inc(sem("w_o"), 1)

            def layer_norm(t, src, st, mv, name):
                nc.vector.bn_stats(st[t.half][:], src).then_inc(sem(name + "_st"), 1)
                ready(dve, name + "_st", t)
                settle(dve)
                nc.vector.bn_aggr(mv[t.half][:], st[t.half][:]).then_inc(sem(name + "_mv"), 1)

            def scale_rows(t, src, dst, mv, rs, name, done):
                ready(dve, name + "_rs", t)
                nc.vector.tensor_scalar(dst, src, mv[t.half][:, 0:1], rs[t.half][:, 0:1],
                                        ALU.subtract, ALU.mult).then_inc(sem(done), 1)

            def ln1(t):
                landed(dve, "x_in", t)
                freed(dve, "ln1_rs", t)
                layer_norm(t, xin[t.half][:], st1, mv1, "ln1")

            def ln1_rows(t):
                freed(dve, "xT_ps", t)
                scale_rows(t, xin[t.half][:], xn[t.half][:], mv1, rs1, "ln1", "ln1")

            def gate(t):
                ready(dve, "o_turned", t)
                ready(dve, "tg", t)
                freed(dve, "on", t)
                nc.vector.scalar_tensor_tensor(out=og[t.half][:], in0=tg[t.half][:], scalar=1.0,
                                               in1=M[:, 0:D], op0=ALU.add, op1=ALU.mult).then_inc(sem("og"), 1)

            def apply_decay(g):
                def part(t):
                    dve.wait_ge(sem("scored"), t.index() * 4 + g + 1)
                    freed(dve, "pv", t, back=1, per=4, at=g + 1)
                    if t.known() and t.index() == 0:
                        dve.wait_ge(sem("decay"), 1)
                    nc.vector.tensor_tensor(probs[:, 4 * g:4 * g + 4, :].rearrange("p h c -> p (h c)"), SC[g % 2][:, :],
                                            decay[:, 4 * g:4 * g + 4, :].rearrange("p h c -> p (h c)"), ALU.mult).then_inc(sem("probs"), 1)
                return part

            def state_out(t):
                if t.half == 0:
                    dve.wait_ge(sem("state_ps"), t.pair + 1)
                    if not (t.known() and t.index() == 0):
                        dve.wait_ge(sem("pv"), t.pair * 8)
                    nc.vector.tensor_tensor(state[:], OT[:, D:2 * D].rearrange("p (c e) -> p c e", c=KC),
                                            same_head[:].rearrange("p (a e) -> p a e", a=1).broadcast_to([P, KC, P]),
                                            ALU.mult).then_inc(sem("state"), 1)

            def head_sums(t):
                p = t.half
                ready(dve, "sq", t)
                freed(dve, "hroot", t)
                nc.vector.tensor_reduce(hsum[p][:], sq[p][:].rearrange("p (h d) -> p h d", d=HD), AX.X,
                                        ALU.add).then_inc(sem("hsum"), 1)
                ready(dve, "hsum", t)
                nc.vector.tensor_scalar(hmean[p][:], hsum[p][:], 1.0 / HD, 4 * EPS, ALU.mult, ALU.add).then_inc(sem("hmean"), 1)
                ready(dve, "hmean", t)
                nc.vector.tensor_scalar(hbits[p][:], hmean[p][:].bitcast(U32), 1, None, ALU.logical_shift_right).then_inc(sem("hbits"), 1)
                ready(dve, "hbits", t)
                nc.vector.tensor_scalar(hguess[p][:], hbits[p][:], -1.0, float(0x5F3759DF), ALU.mult, ALU.add).then_inc(sem("hguess"), 1)

            def square_root1(t):
                p = t.half
                ready(dve, "hguess", t)
                y = hguess[p][:].bitcast(F32)
                nc.vector.tensor_tensor(hsq[p][:], y, y, ALU.mult).then_inc(sem("hsq1"), 1)

            def times_mean1(t):
                p = t.half
                ready(dve, "hsq1", t)
                nc.vector.scalar_tensor_tensor(out=hstep[p][:], in0=hsq[p][:], scalar=-0.5, in1=hmean[p][:],
                                               op0=ALU.mult, op1=ALU.mult).then_inc(sem("hstep1"), 1)

            def root1(t):
                p = t.half
                ready(dve, "hstep1", t)
                nc.vector.scalar_tensor_tensor(out=hfirst[p][:], in0=hstep[p][:], scalar=1.5, in1=hguess[p][:].bitcast(F32),
                                               op0=ALU.add, op1=ALU.mult).then_inc(sem("hfirst"), 1)

            def square_root2(t):
                p = t.half
                ready(dve, "hfirst", t)
                nc.vector.tensor_tensor(hsq[p][:], hfirst[p][:], hfirst[p][:], ALU.mult).then_inc(sem("hsq2"), 1)

            def times_mean2(t):
                p = t.half
                ready(dve, "hsq2", t)
                nc.vector.tensor_tensor(hstep[p][:], hsq[p][:], hmean[p][:], ALU.mult).then_inc(sem("hstep2"), 1)

            def polynomial(t):
                p = t.half
                ready(dve, "hstep2", t)
                nc.vector.scalar_tensor_tensor(out=hpoly[p][:], in0=hstep[p][:], scalar=-10.0 / 3.0, in1=hstep[p][:],
                                               op0=ALU.add, op1=ALU.mult).then_inc(sem("hpoly"), 1)

            def root2(t):
                p = t.half
                ready(dve, "hpoly", t)
                freed(dve, "on", t)
                nc.vector.scalar_tensor_tensor(out=hroot[p][:], in0=hpoly[p][:], scalar=5.0, in1=hfirst[p][:],
                                               op0=ALU.add, op1=ALU.mult).then_inc(sem("hroot"), 1)

            def normalise(t):
                ready(dve, "hroot", t)
                freed(dve, "on_turned", t)
                nc.vector.tensor_tensor(on[t.half][:].rearrange("p (h d) -> p h d", d=HD),
                                        og[t.half][:].rearrange("p (h d) -> p h d", d=HD),
                                        hroot[t.half][:].rearrange("p (h a) -> p h a", a=1).broadcast_to([P, H, HD]),
                                        ALU.mult).then_inc(sem("on"), 1)

            def residual_ln2(t):
                ready(dve, "attn_ps", t)
                landed(dve, "res_in", t)
                res = pay[t.half][:, D:2 * D]
                nc.vector.tensor_tensor(res, res, M[:, D:2 * D], ALU.add).then_inc(sem("x1"), 1)
                ready(dve, "x1", t)
                freed(dve, "ln2_rs", t)
                layer_norm(t, res, st2, mv2, "ln2")

            def ln2_rows(t):
                scale_rows(t, pay[t.half][:, D:2 * D], pay[t.half][:, 0:D], mv2, rs2, "ln2", "x2n")

            def choose(t):
                p = t.half
                ready(dve, "th", t)
                nc.vector.tensor_scalar(route[p][:], th[p][:], 0.5, 0.5, ALU.mult, ALU.add).then_inc(sem("route"), 1)
                ready(dve, "route", t)
                best = pay[p][:, ROW - 2:ROW - 1]
                nc.vector.tensor_reduce(best, route[p][:], AX.X, ALU.max).then_inc(sem("best"), 1)
                ready(dve, "best", t)
                nc.vector.scalar_tensor_tensor(out=cand[p][:], in0=route[p][:], scalar=best, in1=desc[:],
                                               op0=ALU.is_equal, op1=ALU.mult).then_inc(sem("cand"), 1)
                ready(dve, "cand", t)
                nc.vector.tensor_reduce(cmax[p][:], cand[p][:], AX.X, ALU.max).then_inc(sem("cmax"), 1)
                ready(dve, "cmax", t)
                freed(dve, "rank_ps", t)
                nc.vector.tensor_scalar(mask[p][:], cand[p][:], cmax[p][:, 0:1], None, ALU.is_equal).then_inc(sem("mask"), 1)

            def place(t):
                p = t.half
                ready(dve, "rank_ps", t)
                nc.vector.tensor_tensor(rank[p][:], M[:, 16:16 + E], base[:], ALU.add).then_inc(sem("rank"), 1)
                nc.vector.tensor_tensor(seen[:], seen[:], mask[p][:], ALU.add).then_inc(sem("seen"), 1)
                ready(dve, "rank", t)
                nc.vector.tensor_tensor(prod[p][:], rank[p][:], mask[p][:], ALU.mult).then_inc(sem("prod"), 1)
                ready(dve, "prod", t)
                nc.vector.tensor_reduce(posf[p][:], prod[p][:], AX.X, ALU.add).then_inc(sem("posf"), 1)
                ready(dve, "posf", t)
                if not (t.known() and t.index() < 2):
                    dve.wait_ge(sem(f"sorted{p}"), t.pair * 16)
                nc.vector.tensor_copy(pos[p][:], posf[p][:]).then_inc(sem("pos"), 1)

            dve.wait_ge(sem("ones"), 5)
            dve.wait_ge(sem("sh"), 3)
            for a in range(2):
                nc.vector.tensor_reduce(parity[:, a:a + 1], same_head[:, HD * a:P:2 * HD], AX.X, ALU.add).then_inc(sem("parity"), 1)
            first_roots = [(square_root1, -1), (times_mean1, -1), (root1, -1)]
            roots = [(square_root2, -1), (times_mean2, -1), (polynomial, -1), (root2, -1)]
            pipeline(dve, [(ln1, 2), (ln2_rows, -2), (gate, -1), (ln1_rows, 2), (apply_decay(0), 0), (head_sums, -1),
                           *first_roots, (apply_decay(1), 0), (state_out, 0), *roots, (apply_decay(2), 0), (choose, -2), (normalise, -1),
                           (apply_decay(3), 0), (place, -2), (residual_ln2, -1)])

            links = [0]

            def link(ins):
                links[0] += 1
                ins.then_inc(sem("table_step"), 1)
                dve.wait_ge(sem("table_step"), links[0])

            dve.wait_ge(sem("counts_ps"), 1)
            dve.wait_ge(sem("consts"), 4)
            link(nc.vector.tensor_copy(cnt[:], M[0:1, 32:32 + E]))
            link(nc.vector.tensor_tensor(fill_f[:], cnt[:], base[0:1, :], ALU.add))
            nc.vector.tensor_copy(fill_row[:], fill_f[:]).then_inc(sem("fill_row"), 1)
            link(nc.vector.tensor_tensor(over[:], cnt[:].rearrange("p (e a) -> p e a", a=1).broadcast_to([1, E, T]), steps[:], ALU.is_gt))
            link(nc.vector.tensor_reduce(need[:], over[:], AX.X, ALU.add))
            link(nc.vector.tensor_tensor_scan(last[:], need[:], zero_row[:], 0.0, ALU.add, ALU.add))
            link(nc.vector.tensor_tensor(first[:], last[:], need[:], ALU.subtract))

            def over_slots(row):
                return row.rearrange("p (a e) -> p a e", a=1).broadcast_to([1, SLOTS, E])

            link(nc.vector.tensor_tensor(t_ge[:], slot_no[:], over_slots(first[:]), ALU.is_ge))
            link(nc.vector.tensor_tensor(t_in[:], slot_no[:], over_slots(last[:]), ALU.is_lt))
            link(nc.vector.tensor_tensor(t_own[:], t_ge[:], t_in[:], ALU.mult))
            link(nc.vector.tensor_tensor(t_row[:], slot_no[:], over_slots(first[:]), ALU.subtract))
            link(nc.vector.tensor_scalar(t_row2[:], t_row[:], float(P), float(-E * ROOM), ALU.mult, ALU.add))
            link(nc.vector.tensor_tensor(t_row[:], t_row2[:], over_slots(base[0:1, :]), ALU.add))
            link(nc.vector.tensor_tensor(t_val[:], t_row[:], t_own[:], ALU.mult))
            link(nc.vector.tensor_reduce(r_sum[:], t_val[:], AX.X, ALU.add))
            nc.vector.tensor_scalar(slot_row[:], r_sum[:], float(E * ROOM), None, ALU.add).then_inc(sem("slot_row"), 1)
            link(nc.vector.tensor_tensor(t_wt[:], t_own[:], over_slots(woff_e[:]), ALU.mult))
            link(nc.vector.tensor_reduce(w_sum[:], t_wt[:], AX.X, ALU.add))
            nc.vector.tensor_copy(slot_w[:], w_sum[:]).then_inc(sem("slot_w"), 1)

            def hidden(s):
                ready(dve, "up_ps", s)
                ready(dve, "sg", s)
                freed(dve, "hT_ps", s)
                nc.vector.tensor_tensor(hh[s.half][:], sg[s.half][:], SC1[:, :], ALU.mult).then_inc(sem("hh"), 1)

            def combine(s):
                ready(dve, "down_ps", s)
                landed(dve, "rest_in", s)
                if not (s.known() and s.index() < 2):
                    dve.wait_ge(sem(f"stored{s.half}"), s.pair * 16)
                nc.vector.tensor_copy(tok_u[s.half][:], rest[s.half][:, D + 1:D + 2].bitcast(U32)).then_inc(sem("tok_u"), 1)
                ready(dve, "tok_u", s)
                nc.vector.scalar_tensor_tensor(out=yo[s.half][:], in0=M[:, 0:D], scalar=rest[s.half][:, D:D + 1],
                                               in1=rest[s.half][:, 0:D], op0=ALU.mult, op1=ALU.add).then_inc(sem("yo"), 1)

            expert_pipeline(dve, [(hidden, 0), (combine, -1)])

        @block.tensor
        def _(pe):
            pe.wait_ge(sem("ident"), 1)
            pe.wait_ge(sem("ld_exp"), 1)
            for c in range(KC):
                nc.tensor.transpose(TR[:, c * P:(c + 1) * P], ld_exp[:, c * P:(c + 1) * P], ident[:]).then_inc(sem("ld_T"), 1)
            pe.wait_ge(sem("w_g12_in"), 32)
            for c in range(KC):
                ins = nc.tensor.matmul(M[:, c * D:(c + 1) * D], w_g1T[:, c * P:(c + 1) * P], w_g2[:, :], start=True, stop=True)
            ins.then_inc(sem("w_g_ps"), 1)

            def x_turn(t):
                ready(pe, "ln1", t)
                freed(pe, "onT", t, back=3)
                for c in range(KC):
                    ins = nc.tensor.transpose(XT[:, c * P:(c + 1) * P], xn[t.half][:, c * P:(c + 1) * P], ident[:])
                ins.then_inc(sem("xT_ps"), 1)

            def qk_proj(t):
                ready(pe, "xT", t)
                freed(pe, "qk_silu", t, back=1)
                if t.known() and t.index() == 0:
                    pe.wait_ge(sem("w_qk_in"), 32)
                for c in range(KC):
                    ins = nc.tensor.matmul(PJ0[:, :], xT[t.half][:, c, :], w_qkvg[:, c, 0:2 * D], start=(c == 0), stop=(c == KC - 1))
                ins.then_inc(sem("qk_ps"), 1)

            def vg_proj(t):
                freed(pe, "tg", t, back=1)
                if t.known() and t.index() == 0:
                    pe.wait_ge(sem("w_v_in"), 16)
                    pe.wait_ge(sem("w_g"), 1)
                for c in range(KC):
                    ins = nc.tensor.matmul(PJ1[:, :], xT[t.half][:, c, :], w_qkvg[:, c, 2 * D:4 * D], start=(c == 0), stop=(c == KC - 1))
                ins.then_inc(sem("vg_ps"), 1)

            def qk_turn(t):
                ready(pe, "qk_silu", t)
                freed(pe, "qkT", t, back=1)
                if t.known() and t.index() == 0:
                    pe.wait_ge(sem("ld_col"), KC)
                for c in range(2 * KC):
                    ins = nc.tensor.transpose(TR[:, c * P:(c + 1) * P], qk[t.half][:, c * P:(c + 1) * P], ident[:])
                ins.then_inc(sem("qkT_ps"), 1)

            def score(g):
                def part(t):
                    if g == 0:
                        ready(pe, "qkT", t)
                    freed(pe, "probs", t, back=1, per=4, at=g + 3)
                    c, h = g // 2, 4 * (g % 2)
                    nc.tensor.matmul(SC[g % 2][:, :], qkT[t.half][:, KC + c, :],
                                     q_blocks[t.half][:, c, h:h + 4, :].rearrange("p h c -> p (h c)"),
                                     start=True, stop=True).then_inc(sem("scored"), 1)
                return part

            def state_product(t):
                if t.half == 0:
                    pe.wait_ge(sem("kd"), t.pair + 1)
                    ready(pe, "v", t, KC)
                    freed(pe, "oT", t, back=1)
                    for c in range(KC):
                        ins = nc.tensor.matmul(OT[:, D + c * P:D + (c + 1) * P], kd[:, c * P:(c + 1) * P], v_heads(vx[0], c),
                                               start=True, stop=True)
                    ins.then_inc(sem("state_ps"), 1)

            def pv(g):
                def part(t):
                    c = g // 2
                    if g == 0:
                        ready(pe, "v", t, KC)
                        freed(pe, "oT", t, back=1)
                        pe.wait_ge(sem("state"), t.pair + 1)
                        if t.half == 1:
                            pe.wait_ge(sem("qd"), t.pair + 1)
                    if t.half == 1 and g % 2 == 0:
                        nc.tensor.matmul(OT[:, c * P:(c + 1) * P], state[:, c, :], qd[:, c, :], start=True, stop=False,
                                         skip_group_check=True)
                    pe.wait_ge(sem("probs"), t.index() * 4 + g + 1)
                    for a in range(2):
                        for j in (2 * (g % 2), 2 * (g % 2) + 1):
                            head = c * HPC + 2 * j + a
                            ins = nc.tensor.matmul(OT[32 * j:32 * j + 32, c * P:(c + 1) * P], vx[t.half][:, c * HPC // 2 + j, a, :],
                                                   probs[:, head, :], start=(a == 0 and t.half == 0), stop=(a == 1),
                                                   skip_group_check=True)
                    ins.then_inc(sem("pv"), 1)
                return part

            def o_turn(t):
                ready(pe, "oT", t)
                freed(pe, "x1", t, back=1)
                for c in range(KC):
                    ins = nc.tensor.transpose(M[:, c * P:(c + 1) * P], oT[t.half][:, c, :], ident[:])
                ins.then_inc(sem("o_turned"), 1)

            def on_turn(t):
                ready(pe, "on", t)
                freed(pe, "x2T", t, back=1)
                ready(pe, "xT", t.later(2)) if not (t.known() and t.index() >= T - 2) else None
                for c in range(KC):
                    ins = nc.tensor.transpose(XT[:, c * P:(c + 1) * P], on[t.half][:, c * P:(c + 1) * P], ident[:])
                ins.then_inc(sem("on_turned"), 1)

            def attn_out(t):
                ready(pe, "onT", t)
                freed(pe, "rank", t, back=1)
                if t.known() and t.index() == 0:
                    pe.wait_ge(sem("w_o"), KC)
                for c in range(KC):
                    ins = nc.tensor.matmul(M[:, D:2 * D], onT[t.half][:, c, :], w_o[:, c, :], start=(c == 0), stop=(c == KC - 1))
                ins.then_inc(sem("attn_ps"), 1)

            def x2_turn(t):
                ready(pe, "x2n", t)
                if not (t.known() and t.index() >= T - 3):
                    ready(pe, "xT", t.later(3))
                else:
                    ready(pe, "onT", t)
                for c in range(KC):
                    ins = nc.tensor.transpose(XT[:, D + c * P:D + (c + 1) * P], pay[t.half][:, c * P:(c + 1) * P], ident[:])
                ins.then_inc(sem("x2T_ps"), 1)

            def logits(t):
                ready(pe, "x2T", t)
                if not (t.known() and t.index() == T - 1):
                    ready(pe, "og", t.later(1))
                if t.known() and t.index() == 0:
                    pe.wait_ge(sem("w_r_in"), 16)
                for c in range(KC):
                    ins = nc.tensor.matmul(M[:, 0:E], x2T[t.half][:, c, :], w_r[:, c, :], start=(c == 0), stop=(c == KC - 1))
                ins.then_inc(sem("logits_ps"), 1)

            def ranks(t):
                ready(pe, "mask", t)
                freed(pe, "seen", t, back=1)
                nc.tensor.matmul(M[:, 16:16 + E], upper[:], mask[t.half][:], start=True, stop=False)
                nc.tensor.matmul(M[:, 16:16 + E], ones_bf[:], seen[:], start=False, stop=True).then_inc(sem("rank_ps"), 1)

            pipeline(pe, [(x_turn, 1), (score(0), 0), (o_turn, -1), (qk_proj, 1), (score(1), 0), (state_product, 0),
                          (x2_turn, -2), (vg_proj, 1), (logits, -2), (qk_turn, 1), (score(2), 0), (pv(0), 0),
                          (score(3), 0), (ranks, -2), (pv(1), 0), (on_turn, -1), (pv(2), 0), (attn_out, -1), (pv(3), 0)])

            pe.wait_ge(sem("seen"), T)
            pe.wait_ge(sem("rank"), T)
            nc.tensor.matmul(M[0:1, 32:32 + E], ones_bf[:, 0:1], seen[:], start=True, stop=True).then_inc(sem("counts_ps"), 1)

            pe.wait_ge(sem("w_exp"), 16 * 3 * E)
            pe.wait_ge(sem("slot_w"), 1)

            def weights_of(s):
                settle(pe)
                return nc.tensor.value_load(slot_w[0:1, bass.ds(s.index(), 1)], min_val=0, max_val=(E - 1) * EW)

            def xs_turn(s):
                landed(pe, "xs_in", s)
                freed(pe, "xsT", s, back=1)
                for c in range(KC):
                    ins = nc.tensor.transpose(XT[:, c * P:(c + 1) * P], xs[s.half][:, c * P:(c + 1) * P], ident[:])
                ins.then_inc(sem("xsT_ps"), 1)

            def gate2(s):
                ready(pe, "xsT", s)
                freed(pe, "sg", s, back=1)
                w = weights_of(s)
                for c in range(KC):
                    ins = nc.tensor.matmul(SC0[:, :], xsT[s.half][:, c, :], w_exp[:, bass.ds(w + c * F, F)],
                                           start=(c == 0), stop=(c == KC - 1))
                ins.then_inc(sem("gate2_ps"), 1)

            def up2(s):
                freed(pe, "hh", s, back=1)
                w = weights_of(s)
                for c in range(KC):
                    ins = nc.tensor.matmul(SC1[:, :], xsT[s.half][:, c, :], w_exp[:, bass.ds(w + (KC + c) * F, F)],
                                           start=(c == 0), stop=(c == KC - 1))
                ins.then_inc(sem("up_ps"), 1)

            def h_turn(s):
                ready(pe, "hh", s)
                freed(pe, "hT", s, back=1)
                for c in range(FC):
                    ins = nc.tensor.transpose(TR[:, c * P:(c + 1) * P], hh[s.half][:, c * P:(c + 1) * P], ident[:])
                ins.then_inc(sem("hT_ps"), 1)

            def down(s):
                ready(pe, "hT", s)
                freed(pe, "yo", s, back=1)
                w = weights_of(s)
                for c in range(FC):
                    ins = nc.tensor.matmul(M[:, 0:D], hT[s.half][:, c, :], w_exp[:, bass.ds(w + GU + c * D, D)],
                                           start=(c == 0), stop=(c == FC - 1))
                ins.then_inc(sem("down_ps"), 1)

            expert_pipeline(pe, [(gate2, 0), (h_turn, -1), (up2, 0), (xs_turn, 1), (down, -1)])


_INS = ["L0_attn_x", "L0_attn_log_decay", "L0_attn_Wq", "L0_attn_Wk", "L0_attn_Wv", "L0_attn_Wo", "L0_attn_Wg1",
        "L0_attn_Wg2", "L0_attn_norm_w", "L0_ffn_router_w", "L0_ffn_gate_w", "L0_ffn_up_w", "L0_ffn_down_w"]


def kernel(**inputs):
    import numpy as np
    import concourse.bacc as bacc
    from concourse.bass_utils import run_bass_kernel_spmd

    nc = bacc.Bacc("TRN2", target_bir_lowering=False, num_devices=1)
    arrays, args = {}, []
    for name in _INS:
        a = np.ascontiguousarray(inputs[name])
        arrays[f"in_{name}"] = a
        args.append(nc.dram_tensor(f"in_{name}", a.shape, mybir.dt.from_np(a.dtype), kind="ExternalInput").ap())
    out = nc.dram_tensor("out", inputs["L0_attn_x"].shape, F32, kind="ExternalOutput").ap()
    lightning_block(nc, *args, out)
    r = run_bass_kernel_spmd(nc, [arrays], core_ids=[0])
    return r.results[0]["out"]
```

```python
from contextlib import ExitStack

import concourse.bass as bass
from concourse import mybir

ALU = mybir.AluOpType
ACT = mybir.ActivationFunctionType
AX = mybir.AxisListType
F32 = mybir.dt.float32
BF16 = mybir.dt.bfloat16
I32 = mybir.dt.int32
U32 = mybir.dt.uint32
F32R = mybir.dt.float32r

P = 128
EPS = 1e-5


class Tile:

    def __init__(self, pair, half):
        self.pair, self.half = pair, half

    def index(self):
        return self.pair * 2 + self.half

    def later(self, n):
        return Tile(self.pair + (self.half + n) // 2, (self.half + n) % 2)

    def known(self):
        return isinstance(self.pair, int)


def lightning_block(nc, x, log_decay, wq, wk, wv, wo, wg1, wg2, norm_w, router_w, gate_w, up_w, down_w, out):
    B, N, D = x.shape
    H = log_decay.shape[0]
    HD = D // H
    E, _, F = gate_w.shape
    T = B * N // P
    KC = D // P
    FC = F // P
    HPC = P // HD
    SLOTS = T + E - 1
    ROOM = B * N + P
    ROWS = E * ROOM + P
    GU = 2 * KC * F
    EW = GU + FC * D
    REST = D + 2
    ROW = D + REST
    SKIP = 1 << 20
    assert N == 2 * P and D == 2 * P and F == 512 and H * HD == D and HD == 16

    x_rows = x.rearrange("b n d -> (b n) d")
    out_rows = out.rearrange("b n d -> (b n) d")
    sorted_rows = nc.dram_tensor("sorted_rows", (ROWS, ROW), F32, kind="Internal").ap()

    with ExitStack() as ctx:
        def sb(name, shape, dt=F32):
            return ctx.enter_context(nc.sbuf_tensor(name, shape, dt))

        def ps(name):
            return ctx.enter_context(nc.psum_tensor(name, [P, 512], F32))

        sems = {}

        def sem(name):
            if name not in sems:
                sems[name] = ctx.enter_context(nc.semaphore(name))
            return sems[name]

        w_exp = sb("w_exp", [P, E * EW])
        w_qkvg = sb("w_qkvg", [P, KC, 4 * D], F32R)
        w_qkvg_low = sb("w_qkvg_low", [P, KC, 4 * D], F32R)
        w_o = sb("w_o", [P, KC, D], F32R)
        w_o_low = sb("w_o_low", [P, KC, D], F32R)
        w_raw = w_exp[:, (E - 1) * EW:(E - 1) * EW + KC * 4 * D].rearrange("p (c e) -> p c e", c=KC)
        w_g1T = sb("w_g1T", [HD, D])
        w_g2 = sb("w_g2", [HD, D])
        w_r = sb("w_r", [P, KC, E])
        nw = sb("nw", [P, KC])
        ident = sb("ident", [P, P])
        upper = sb("upper", [P, P], BF16)
        ones_bf = sb("ones_bf", [P, P], BF16)
        same_head = sb("same_head", [P, P])
        neg_half = sb("neg_half", [P, H])
        parity = sb("parity", [P, 2])
        ld_row = sb("ld_row", [P, H])
        ld_exp = sb("ld_exp", [P, D])
        ld_col = sb("ld_col", [P, KC])
        dist = sb("dist", [P, P])
        ahead = sb("ahead", [P, P])
        behind = sb("behind", [P, 1])
        decay = sb("decay", [P, H, P])
        k_decay = sb("k_decay", [P, D])
        q_decay = sb("q_decay", [P, KC, P])
        desc = sb("desc", [P, E])
        base = sb("base", [P, E])
        pad_row = sb("pad_row", [P, ROW])
        xin = [sb(f"xin{i}", [P, D]) for i in range(2)]
        xn = [sb(f"xn{i}", [P, D]) for i in range(2)]
        xT = [sb(f"xT{i}", [P, KC, P], F32R) for i in range(2)]
        xT_low = [sb(f"xT_low{i}", [P, KC, P], F32R) for i in range(2)]
        st1 = [sb(f"st1{i}", [P, 6]) for i in range(2)]
        mv1 = [sb(f"mv1{i}", [P, 2]) for i in range(2)]
        ve1 = [sb(f"ve1{i}", [P, 1]) for i in range(2)]
        rs1 = [sb(f"rs1{i}", [P, 1]) for i in range(2)]
        qk = [sb(f"qk{i}", [P, 2 * D]) for i in range(2)]
        vx = [sb(f"vx{i}", [P, H // 2, 2, 2 * HD]) for i in range(2)]
        tg = [sb(f"tg{i}", [P, D]) for i in range(2)]
        qkT = [sb(f"qkT{i}", [P, 2 * KC, P]) for i in range(2)]
        q_blocks = [sb(f"q_blocks{i}", [P, KC, HPC, P]) for i in range(2)]
        kd = sb("kd", [P, D])
        qd = sb("qd", [P, KC, P])
        state = sb("state", [P, KC, P])
        probs = sb("probs", [P, H, P])
        og = [sb(f"og{i}", [P, D]) for i in range(2)]
        sq = [sb(f"sq{i}", [P, D]) for i in range(2)]
        oT = [sb(f"oT{i}", [P, KC, P]) for i in range(2)]
        hsum = [sb(f"hsum{i}", [P, H]) for i in range(2)]
        hmean = [sb(f"hmean{i}", [P, H]) for i in range(2)]
        hbits = [sb(f"hbits{i}", [P, H], U32) for i in range(2)]
        hguess = [sb(f"hguess{i}", [P, H], I32) for i in range(2)]
        hsq = [sb(f"hsq{i}", [P, H]) for i in range(2)]
        hstep = [sb(f"hstep{i}", [P, H]) for i in range(2)]
        hfirst = [sb(f"hfirst{i}", [P, H]) for i in range(2)]
        hpoly = [sb(f"hpoly{i}", [P, H]) for i in range(2)]
        hroot = [sb(f"hroot{i}", [P, H]) for i in range(2)]
        on = [sb(f"on{i}", [P, D]) for i in range(2)]
        onT = [sb(f"onT{i}", [P, KC, P], F32R) for i in range(2)]
        onT_low = [sb(f"onT_low{i}", [P, KC, P], F32R) for i in range(2)]
        st2 = [sb(f"st2{i}", [P, 6]) for i in range(2)]
        mv2 = [sb(f"mv2{i}", [P, 2]) for i in range(2)]
        ve2 = [sb(f"ve2{i}", [P, 1]) for i in range(2)]
        rs2 = [sb(f"rs2{i}", [P, 1]) for i in range(2)]
        pay = [sb(f"pay{i}", [P, ROW]) for i in range(2)]
        x2T = [sb(f"x2T{i}", [P, KC, P]) for i in range(2)]
        th = [sb(f"th{i}", [P, E]) for i in range(2)]
        route = [sb(f"route{i}", [P, E]) for i in range(2)]
        cand = [sb(f"cand{i}", [P, E]) for i in range(2)]
        cmax = [sb(f"cmax{i}", [P, 1]) for i in range(2)]
        mask = [sb(f"mask{i}", [P, E], BF16) for i in range(2)]
        seen = sb("seen", [P, E], BF16)
        rank = [sb(f"rank{i}", [P, E]) for i in range(2)]
        prod = [sb(f"prod{i}", [P, E]) for i in range(2)]
        posf = [sb(f"posf{i}", [P, 1]) for i in range(2)]
        pos = [sb(f"pos{i}", [P, 1], U32) for i in range(2)]
        tok = sb("tok", [P, 1], I32)
        cnt = sb("cnt", [1, E])
        steps = sb("steps", [1, E, T])
        over = sb("over", [1, E, T])
        need = sb("need", [1, E])
        zero_row = sb("zero_row", [1, E])
        last = sb("last", [1, E])
        way = sb("way", [1, E])
        way_e = sb("way_e", [1, E])
        slot_start = sb("slot_start", [1, SLOTS])
        slot_no = sb("slot_no", [1, SLOTS, E])
        table = decay[0:1, :, :].rearrange("p h c -> p (h c)")
        t_behind, t_way = [table[:, i * SLOTS * E:(i + 1) * SLOTS * E].rearrange("p (s e) -> p s e", e=E) for i in range(2)]
        r_sum = sb("r_sum", [1, SLOTS])
        w_sum = sb("w_sum", [1, SLOTS])
        slot_row = sb("slot_row", [1, SLOTS], I32)
        slot_w = sb("slot_w", [1, SLOTS], I32)
        fill_f = sb("fill_f", [1, E])
        fill_row = sb("fill_row", [1, E], I32)
        tok_u = [sb(f"tok_u{i}", [P, 1], U32) for i in range(2)]
        xsT = [sb(f"xsT{i}", [P, KC, P]) for i in range(2)]
        xs = xin
        rest = [qk[i][:, 0:REST] for i in range(2)]
        hT = [probs[:, FC * i:FC * (i + 1), :] for i in range(2)]
        sg = [probs[:, FC * (i + 2):FC * (i + 3), :].rearrange("p c t -> p (c t)") for i in range(2)]
        hh = [q_blocks[i][:, 0, 0:FC, :].rearrange("p c t -> p (c t)") for i in range(2)]
        yo = on

        PJ0, PJ1, TR, XT, SC0, SC1, OT, M = [ps(n) for n in ("PJ0", "PJ1", "TR", "XT", "SC0", "SC1", "OT", "M")]
        SC = [SC0, SC1]

        def v_heads(buf, c):
            pairs = HPC // 2
            flat = buf[:, c * pairs:(c + 1) * pairs, :, :].rearrange("p j a b -> p j (a b)")
            both = flat.rearrange("p j (a b) -> p j b a", a=4)[:, :, :, 0:4:3]
            return both.rearrange("p j b a -> p j a b")

        block = ctx.enter_context(nc.Block())

        def ready(eng, name, tile, per=1, extra=0):
            eng.wait_ge(sem(name), tile.index() * per + per + extra)

        def settle(eng):
            eng.sem_inc(sem("waited"), 1)

        def landed(eng, name, tile, n=1):
            eng.wait_ge(sem(f"{name}{tile.half}"), tile.pair * 16 * n + 16 * n)

        def freed(eng, name, tile, back=2, per=1, at=None):
            n = (tile.index() - back) * per + (per if at is None else at)
            if isinstance(n, int) and n <= 0:
                return
            eng.wait_ge(sem(name), n)

        def run_steps(eng, step, lo, hi):
            n = lo
            while n < hi:
                if n == 4:
                    with eng.Fori(2, (T - 2) // 2) as pair:
                        for half in range(2):
                            step(Tile(pair, half), None)
                    n = T - 2
                else:
                    step(Tile(n // 2, n % 2), n)
                    n += 1

        def valid(tile, n, shift):
            return n is None or 0 <= n + shift < T

        def pipeline(eng, parts):
            def step(tile, n):
                for part, shift in parts:
                    if valid(tile, n, shift):
                        part(tile.later(shift))
            run_steps(eng, step, -2, T + 2)

        def expert_pipeline(eng, parts):
            def step(s, n):
                for part, shift in parts:
                    if n is None or 0 <= n + shift < SLOTS:
                        part(s.later(shift))
            for n in range(-1, 4):
                step(Tile(n // 2, n % 2), n)
            with eng.Fori(2, (SLOTS - 1) // 2) as pair:
                step(Tile(pair, 0), None)
                step(Tile(pair, 1), None)
            for n in (SLOTS - 1, SLOTS):
                step(Tile(n // 2, n % 2), n)

        @block.sync
        def _(sp):
            def load_x(t):
                freed(sp, "ln1", t)
                sp.dma_start(xin[t.half][:, :], x_rows[bass.ds(t.index() * P, P), :]).then_inc(sem(f"x_in{t.half}"), 16)
                if t.known() and t.index() == 0:
                    for i, w in enumerate((wq, wk)):
                        sp.dma_start(w_raw[:, :, i * D:(i + 1) * D], w.rearrange("(c p) e -> p c e", p=P)).then_inc(sem("w_qk_in"), 16)

            def load_residual(t):
                if not (t.known() and t.index() < 2):
                    sp.wait_ge(sem(f"sorted{t.half}"), t.pair * 16)
                sp.dma_start(pay[t.half][:, D:2 * D], x_rows[bass.ds(t.index() * P, P), :]).then_inc(sem(f"res_in{t.half}"), 16)

            def load_expert(t):
                e = bass.ds(t.pair, 1)
                if t.known() and t.pair == E - 1 and t.half == 0:
                    sp.wait_ge(sem("w_qk"), 2)
                    sp.wait_ge(sem("w_v"), 2)
                    sp.wait_ge(sem("w_o"), 3)
                if t.half == 0:
                    for i, w in enumerate((gate_w, up_w)):
                        sp.dma_start(w_exp[:, bass.ds(t.pair * EW + i * KC * F, KC * F)].rearrange("p (c f) -> p c f", c=KC),
                                     w[e, :, :].rearrange("a (c p) f -> p (a c) f", p=P)).then_inc(sem("w_exp"), 16)
                else:
                    sp.dma_start(w_exp[:, bass.ds(t.pair * EW + GU, FC * D)].rearrange("p (c d) -> p c d", c=FC),
                                 down_w[e, :, :].rearrange("a (c p) d -> p (a c) d", p=P)).then_inc(sem("w_exp"), 16)

            pipeline(sp, [(load_x, 2), (load_residual, -1), (load_expert, 0)])

            sp.wait_ge(sem("pad"), 2)
            sp.wait_ge(sem("fill_row"), 1)
            for e in range(0, E, 2):
                r = nc.sync.value_load(fill_row[0:1, e:e + 1], min_val=0, max_val=E * ROOM - P)
                sp.dma_start(sorted_rows[bass.ds(r, P), :], pad_row[:, :]).then_inc(sem("filled"), 16)
            sp.wait_ge(sem("filled"), 16 * E)
            sp.wait_ge(sem("spare_filled"), 16)
            sp.wait_ge(sem("sorted0"), 16 * (T // 2))
            sp.wait_ge(sem("sorted1"), 16 * (T // 2))
            sp.wait_ge(sem("slot_row"), 1)

            def row_of(s):
                return nc.sync.value_load(slot_row[0:1, bass.ds(s.index(), 1)], min_val=0, max_val=E * ROOM)

            def load_xs(s):
                r = row_of(s)
                freed(sp, "xsT_ps", s)
                sp.dma_start(xs[s.half][:, :], sorted_rows[bass.ds(r, P), 0:D]).then_inc(sem(f"xs_in{s.half}"), 16)

            def load_rest(s):
                r = row_of(s)
                freed(sp, "yo", s)
                sp.dma_start(rest[s.half][:, :], sorted_rows[bass.ds(r, P), D:ROW]).then_inc(sem(f"rest_in{s.half}"), 16)

            expert_pipeline(sp, [(load_xs, 1), (load_rest, -1)])

        @block.gpsimd
        def _(pool):
            pool.dma_start(ld_row[:, :], log_decay.rearrange("(a h) -> a h", a=1).broadcast_to([P, H])).then_inc(sem("ld_in"), 16)
            nc.gpsimd.memset(neg_half[:], -0.5).then_inc(sem("neg_half"), 1)
            nc.gpsimd.iota(dist[:], pattern=[[1, P]], base=0, channel_multiplier=-1,
                           allow_small_or_imprecise_dtypes=True).then_inc(sem("dist"), 1)
            nc.gpsimd.iota(ahead[:], pattern=[[1, P]], base=1, channel_multiplier=0,
                           allow_small_or_imprecise_dtypes=True).then_inc(sem("dist"), 1)
            nc.gpsimd.iota(behind[:], pattern=[[0, 1]], base=P - 1, channel_multiplier=-1,
                           allow_small_or_imprecise_dtypes=True).then_inc(sem("dist"), 1)
            pool.wait_ge(sem("dist"), 1)
            nc.gpsimd.tensor_scalar(dist[:], dist[:], 0.0, None, ALU.max).then_inc(sem("dist"), 1)
            nc.gpsimd.memset(ident[:], 0.0).then_inc(sem("zeroed"), 1)
            pool.wait_ge(sem("zeroed"), 1)
            nc.gpsimd.affine_select(out=ident[:], in_=ident[:], compare_op=ALU.not_equal, fill=1.0, base=0,
                                    pattern=[[-1, P]], channel_multiplier=1).then_inc(sem("ident"), 1)

            def decays(t):
                if t.half == 0:
                    ready(pool, "qk_silu", t)
                    pool.wait_ge(sem("k_decay"), 1)
                    if not (t.known() and t.index() == 0):
                        pool.wait_ge(sem("state_ps"), t.pair)
                    nc.gpsimd.tensor_tensor(kd[:], qk[0][:, D:2 * D], k_decay[:], ALU.mult).then_inc(sem("kd"), 1)
                else:
                    ready(pool, "qkT", t)
                    pool.wait_ge(sem("q_decay"), KC)
                    if not (t.known() and t.index() == 1):
                        freed(pool, "pv", t, per=4)
                    nc.gpsimd.tensor_tensor(qd[:], qkT[1][:, 0:KC, :], q_decay[:], ALU.mult).then_inc(sem("qd"), 1)

            def inverse_root(t, dst, mid, src, scale, eps, name):
                nc.gpsimd.tensor_scalar(mid, src, scale, eps, ALU.mult, ALU.add).then_inc(sem(name + "_sum"), 1)
                ready(pool, name + "_sum", t)
                settle(pool)
                nc.gpsimd.tensor_tensor(dst, mid, neg_half[:, 0:dst.shape[1]], ALU.pow).then_inc(sem(name), 1)

            def ln1_root(t):
                ready(pool, "ln1_mv", t)
                freed(pool, "ln1", t)
                settle(pool)
                inverse_root(t, rs1[t.half][:], ve1[t.half][:], mv1[t.half][:, 1:2], 1.0, EPS, "ln1_rs")

            def ln2_root(t):
                ready(pool, "ln2_mv", t)
                freed(pool, "x2n", t)
                settle(pool)
                inverse_root(t, rs2[t.half][:], ve2[t.half][:], mv2[t.half][:, 1:2], 1.0, EPS, "ln2_rs")

            def normalise(t):
                ready(pool, "hroot", t)
                freed(pool, "on_turned", t)
                nc.gpsimd.tensor_tensor(on[t.half][:].rearrange("p (h d) -> p h d", d=HD),
                                        og[t.half][:].rearrange("p (h d) -> p h d", d=HD),
                                        hroot[t.half][:].rearrange("p (h a) -> p h a", a=1).broadcast_to([P, H, HD]),
                                        ALU.mult).then_inc(sem("on"), 1)

            def token_numbers(t):
                if t.known() and t.index() < 2:
                    pool.wait_ge(sem("tok"), 1)
                else:
                    pool.wait_ge(sem(f"sorted{t.half}"), t.pair * 16)
                    ready(pool, "tok", t)
                settle(pool)
                nc.gpsimd.tensor_copy(pay[t.half][:, ROW - 1:ROW].bitcast(I32), tok[:]).then_inc(sem("tok_in"), 1)
                ready(pool, "tok_in", t)
                settle(pool)
                nc.gpsimd.tensor_scalar(tok[:], tok[:], float(P), None, ALU.add).then_inc(sem("tok"), 1)

            def sort(t):
                ready(pool, "pos", t)
                settle(pool)
                pool.indirect_dma_start(out=sorted_rows, out_offset=bass.IndirectOffsetOnAxis(ap=pos[t.half][:, 0:1], axis=0),
                                        in_=pay[t.half][:, :], in_offset=None).then_inc(sem(f"sorted{t.half}"), 16)

            def more_constants(t):
                if not t.known() or t.index() > 2:
                    return
                if t.index() == 0:
                    nc.gpsimd.memset(same_head[:], 1.0).then_inc(sem("sh"), 1)
                    blocks = same_head[:].rearrange("p (h d) -> p h d", d=HD)
                    pool.wait_ge(sem("sh"), 1)
                    nc.gpsimd.affine_select(out=blocks, in_=blocks, compare_op=ALU.is_ge, fill=0.0, base=0,
                                            pattern=[[-HD, HPC], [0, HD]], channel_multiplier=1).then_inc(sem("sh"), 1)
                    pool.wait_ge(sem("sh"), 2)
                    nc.gpsimd.affine_select(out=blocks, in_=blocks, compare_op=ALU.is_ge, fill=0.0, base=HD - 1,
                                            pattern=[[HD, HPC], [0, HD]], channel_multiplier=-1).then_inc(sem("sh"), 1)
                    for i in range(2):
                        nc.gpsimd.memset(q_blocks[i][:], 0.0).then_inc(sem("q_zeroed"), 1)
                        nc.gpsimd.memset(vx[i][:], 0.0).then_inc(sem("v_zeroed"), 1)
                elif t.index() == 1:
                    pool.wait_ge(sem("decay_exp"), 1)
                    nc.gpsimd.affine_select(out=decay[:], in_=decay[:], compare_op=ALU.is_ge, fill=0.0, base=0,
                                            pattern=[[0, H], [1, P]], channel_multiplier=-1).then_inc(sem("decay"), 1)
                else:
                    nc.gpsimd.memset(ones_bf[:], 1.0).then_inc(sem("ones"), 1)
                    pool.wait_ge(sem("ones"), 1)
                    nc.gpsimd.affine_select(out=upper[:], in_=ones_bf[:], compare_op=ALU.is_gt, fill=0.0, base=0,
                                            pattern=[[1, P]], channel_multiplier=-1).then_inc(sem("ones"), 1)
                    nc.gpsimd.memset(seen[:], 0.0).then_inc(sem("ones"), 1)
                    nc.gpsimd.iota(desc[:], pattern=[[-1, E]], base=E, channel_multiplier=0,
                                   allow_small_or_imprecise_dtypes=True).then_inc(sem("ones"), 1)
                    nc.gpsimd.iota(base[:], pattern=[[ROOM, E]], base=0, channel_multiplier=0,
                                   allow_small_or_imprecise_dtypes=True).then_inc(sem("ones"), 1)
                    nc.gpsimd.iota(tok[:], pattern=[[0, 1]], base=0, channel_multiplier=1).then_inc(sem("tok"), 1)
                    nc.gpsimd.iota(steps[:], pattern=[[0, E], [P, T]], base=0, channel_multiplier=0,
                                   allow_small_or_imprecise_dtypes=True).then_inc(sem("consts"), 1)
                    nc.gpsimd.memset(zero_row[:], 0.0).then_inc(sem("consts"), 1)
                    nc.gpsimd.iota(slot_no[:], pattern=[[1, SLOTS], [0, E]], base=0, channel_multiplier=0,
                                   allow_small_or_imprecise_dtypes=True).then_inc(sem("consts"), 1)
                    nc.gpsimd.iota(slot_start[:], pattern=[[P, SLOTS]], base=0, channel_multiplier=0,
                                   allow_small_or_imprecise_dtypes=True).then_inc(sem("consts"), 1)
                    nc.gpsimd.memset(way_e[:, 0:E - 1], float(ROOM)).then_inc(sem("consts"), 1)
                    nc.gpsimd.memset(way_e[:, E - 1:E], float(ROWS)).then_inc(sem("consts"), 1)
                    nc.gpsimd.memset(pad_row[:, 0:ROW - 1], 0.0).then_inc(sem("pad"), 1)
                    nc.gpsimd.memset(pad_row[:, ROW - 1:ROW].bitcast(I32), SKIP).then_inc(sem("pad"), 1)
                    pool.wait_ge(sem("pad"), 2)
                    pool.dma_start(sorted_rows[E * ROOM:ROWS, :], pad_row[:, :]).then_inc(sem("spare_filled"), 16)

            pool.wait_ge(sem("neg_half"), 1)
            pipeline(pool, [(ln1_root, 2), (token_numbers, -2), (normalise, -1), (sort, -2), (ln2_root, -1),
                           (decays, 1), (more_constants, 2)])

            def store(s):
                ready(pool, "yo", s)
                settle(pool)
                pool.indirect_dma_start(out=out_rows, out_offset=bass.IndirectOffsetOnAxis(ap=tok_u[s.half][:, 0:1], axis=0),
                                        in_=yo[s.half][:, :], in_offset=None, bounds_check=B * N - 1,
                                        oob_is_err=False).then_inc(sem(f"stored{s.half}"), 16)
            with pool.Fori(0, SLOTS // 2) as pair:
                store(Tile(pair, 0))
                store(Tile(pair, 1))
            store(Tile(SLOTS // 2, 0))
            pool.wait_ge(sem("stored0"), 16 * (SLOTS // 2 + 1))
            pool.wait_ge(sem("stored1"), 16 * (SLOTS // 2))

        @block.scalar
        def _(act):
            with nc.allow_non_contiguous_dma("4,096 numbers, once"):
                act.dma_start(w_g1T[:, :], wg1.rearrange("d k -> k d")).then_inc(sem("w_g12_in"), 16)
            act.dma_start(w_g2[:, :], wg2).then_inc(sem("w_g12_in"), 16)
            act.dma_start(w_raw[:, :, 2 * D:3 * D], wv.rearrange("(c p) e -> p c e", p=P)).then_inc(sem("w_v_in"), 16)
            act.dma_start(w_raw[:, :, 3 * D:4 * D], wo.rearrange("(c p) e -> p c e", p=P)).then_inc(sem("w_o_in"), 16)
            with nc.allow_non_contiguous_dma("256 numbers, once"):
                act.dma_start(nw[:, :], norm_w.rearrange("(c p) -> p c", p=P)).then_inc(sem("w_o_in"), 16)
            act.dma_start(w_r[:, :, :], router_w.rearrange("(c p) e -> p c e", p=P)).then_inc(sem("w_r_in"), 16)
            act.wait_ge(sem("ld_in"), 16)
            nc.scalar.activation(ld_exp[:].rearrange("p (h d) -> p h d", d=HD),
                                 ld_row[:].rearrange("p (h a) -> p h a", a=1).broadcast_to([P, H, HD]), ACT.Copy).then_inc(sem("ld_exp"), 1)
            act.wait_ge(sem("decay_log"), 1)
            nc.scalar.activation(decay[:], decay[:], ACT.Exp).then_inc(sem("decay_exp"), 1)
            act.wait_ge(sem("ld_exp"), 1)
            nc.scalar.activation(k_decay[:], ld_exp[:], ACT.Exp, scale=behind[:, 0:1]).then_inc(sem("k_decay"), 1)
            act.wait_ge(sem("w_g_ps"), 1)
            nc.scalar.activation(w_qkvg[:, :, 3 * D:4 * D], M[:, :].rearrange("p (c e) -> p c e", c=KC), ACT.Copy).then_inc(sem("w_g"), 1)
            act.wait_ge(sem("ld_T"), KC)
            for c in range(KC):
                nc.scalar.activation(ld_col[:, c:c + 1], TR[:, c * P:c * P + 1], ACT.Copy).then_inc(sem("ld_col"), 1)
            act.wait_ge(sem("ld_col"), KC)
            for c in range(KC):
                nc.scalar.activation(q_decay[:, c, :], ahead[:], ACT.Exp, scale=ld_col[:, c:c + 1]).then_inc(sem("q_decay"), 1)

            def xT_out(t):
                ready(act, "xT_ps", t)
                freed(act, "vg_ps", t)
                nc.scalar.activation(xT[t.half][:].rearrange("p c t -> p (c t)"), XT[:, 0:D], ACT.Copy).then_inc(sem("xT"), 1)

            def oT_out(t):
                ready(act, "pv", t, 4)
                freed(act, "o_turned", t)
                nc.scalar.activation(oT[t.half][:].rearrange("p c t -> p (c t)"), OT[:, 0:D], ACT.Copy).then_inc(sem("oT"), 1)

            def onT_out(t):
                ready(act, "on_turned", t)
                freed(act, "attn_ps", t)
                nc.scalar.activation(onT[t.half][:].rearrange("p c t -> p (c t)"), XT[:, 0:D], ACT.Copy).then_inc(sem("onT"), 1)

            def qk_silu(t):
                ready(act, "qk_ps", t)
                freed(act, "qkT_ps", t)
                if t.half == 0:
                    if not (t.known() and t.index() == 0):
                        act.wait_ge(sem("kd"), t.pair)
                nc.scalar.activation(qk[t.half][:, :], PJ0[:, :], ACT.Silu).then_inc(sem("qk_silu"), 1)

            def v_silu(t):
                ready(act, "vg_ps", t)
                freed(act, "pv", t, per=4)
                if t.known() and t.index() < 2:
                    act.wait_ge(sem("v_zeroed"), 2)
                for c in range(KC):
                    nc.scalar.activation(v_heads(vx[t.half], c),
                                         PJ1[:, c * P:(c + 1) * P].rearrange("p (j a b) -> p j a b", a=2, b=HD),
                                         ACT.Silu).then_inc(sem("v"), 1)
                freed(act, "og", t)
                nc.scalar.activation(tg[t.half][:], PJ1[:, D:2 * D], ACT.Tanh,
                                     scale=0.5).then_inc(sem("tg"), 1)

            def qkT_out(t):
                ready(act, "qkT_ps", t)
                freed(act, "scored", t, per=4)
                if t.half == 1 and not (t.known() and t.index() == 1):
                    act.wait_ge(sem("qd"), t.pair)
                if t.known() and t.index() == 0:
                    act.wait_ge(sem("parity"), 2)
                if t.known() and t.index() < 2:
                    act.wait_ge(sem("q_zeroed"), 2)
                for j in range(HPC // 2):
                    r = slice(32 * j, 32 * j + 32)
                    for a in range(2):
                        nc.scalar.activation(q_blocks[t.half][r, :, 2 * j + a, :], TR[r, 0:D].rearrange("p (c t) -> p c t", c=KC),
                                             ACT.Copy, scale=parity[r, a:a + 1])
                lo = KC if t.half == 0 else 0
                nc.scalar.activation(qkT[t.half][:, lo:, :].rearrange("p c t -> p (c t)"), TR[:, lo * P:], ACT.Copy).then_inc(sem("qkT"), 1)

            def square(t):
                ready(act, "og", t)
                freed(act, "hsum", t)
                nc.scalar.activation(sq[t.half][:], og[t.half][:], ACT.Square).then_inc(sem("sq"), 1)

            def x2T_out(t):
                ready(act, "x2T_ps", t)
                freed(act, "logits_ps", t)
                nc.scalar.activation(x2T[t.half][:].rearrange("p c t -> p (c t)"), XT[:, D:2 * D], ACT.Copy).then_inc(sem("x2T"), 1)

            def logits_tanh(t):
                ready(act, "logits_ps", t)
                freed(act, "route", t)
                nc.scalar.activation(th[t.half][:], M[:, 0:E], ACT.Tanh, scale=0.5).then_inc(sem("th"), 1)

            pipeline(act, [(oT_out, -1), (xT_out, 1), (square, -1), (qk_silu, 1), (x2T_out, -2), (logits_tanh, -2),
                           (qkT_out, 1), (onT_out, -1), (v_silu, 1)])

            act.wait_ge(sem("pad"), 2)
            act.wait_ge(sem("fill_row"), 1)
            for e in range(1, E, 2):
                r = nc.scalar.value_load(fill_row[0:1, e:e + 1], min_val=0, max_val=E * ROOM - P)
                act.dma_start(sorted_rows[bass.ds(r, P), :], pad_row[:, :]).then_inc(sem("filled"), 16)

            def xsT_out(s):
                ready(act, "xsT_ps", s)
                freed(act, "up_ps", s)
                nc.scalar.activation(xsT[s.half][:].rearrange("p c t -> p (c t)"), XT[:, 0:D], ACT.Copy).then_inc(sem("xsT"), 1)

            def h_silu(s):
                ready(act, "gate2_ps", s)
                freed(act, "hh", s)
                nc.scalar.activation(sg[s.half][:], SC0[:, :], ACT.Silu).then_inc(sem("sg"), 1)

            def hT_out(s):
                ready(act, "hT_ps", s)
                freed(act, "down_ps", s)
                nc.scalar.activation(hT[s.half][:].rearrange("p c t -> p (c t)"), TR[:, :], ACT.Copy).then_inc(sem("hT"), 1)

            expert_pipeline(act, [(hT_out, -1), (h_silu, 0), (xsT_out, 1)])

        @block.vector
        def _(dve):
            def low(dst, src, high):
                return nc.vector.tensor_tensor(dst, src, high.bitcast(F32), ALU.subtract)

            def split_weights():
                dve.wait_ge(sem("w_qk_in"), 32)
                nc.vector.tensor_copy(w_qkvg[:, :, 0:2 * D], w_raw[:, :, 0:2 * D]).then_inc(sem("w_qk"), 1)
                dve.wait_ge(sem("w_v_in"), 16)
                nc.vector.tensor_copy(w_qkvg[:, :, 2 * D:3 * D], w_raw[:, :, 2 * D:3 * D]).then_inc(sem("w_v"), 1)
                dve.wait_ge(sem("w_qk"), 1)
                low(w_qkvg_low[:, :, 0:2 * D], w_raw[:, :, 0:2 * D], w_qkvg[:, :, 0:2 * D]).then_inc(sem("w_qk"), 1)
                dve.wait_ge(sem("w_v"), 1)
                low(w_qkvg_low[:, :, 2 * D:3 * D], w_raw[:, :, 2 * D:3 * D], w_qkvg[:, :, 2 * D:3 * D]).then_inc(sem("w_v"), 1)

            def split_more_weights():
                dve.wait_ge(sem("w_g"), 1)
                low(w_qkvg_low[:, :, 3 * D:4 * D], M[:, :].rearrange("p (c e) -> p c e", c=KC),
                    w_qkvg[:, :, 3 * D:4 * D]).then_inc(sem("w_g"), 1)
                w_or = w_raw[:, :, 3 * D:4 * D]
                dve.wait_ge(sem("w_o_in"), 32)
                for c in range(KC):
                    nc.vector.tensor_scalar(w_or[:, c, :], w_or[:, c, :], nw[:, c:c + 1], 3.0 / 8.0, ALU.mult, ALU.mult).then_inc(sem("w_o_scaled"), 1)
                dve.wait_ge(sem("w_o_scaled"), KC)
                nc.vector.tensor_copy(w_o[:, :, :], w_or).then_inc(sem("w_o"), 1)
                dve.wait_ge(sem("w_o"), 1)
                low(w_o_low[:, :, :], w_or, w_o[:, :, :]).then_inc(sem("w_o"), 2)

            def scale_rows(t, src, dst, mv, rs, name, done):
                ready(dve, name + "_rs", t)
                nc.vector.tensor_scalar(dst, src, mv[t.half][:, 0:1], rs[t.half][:, 0:1],
                                        ALU.subtract, ALU.mult).then_inc(sem(done), 1)

            def x_low(t):
                ready(dve, "xT", t)
                freed(dve, "vg_ps", t)
                nc.vector.tensor_tensor(xT_low[t.half][:].rearrange("p c t -> p (c t)"), XT[:, 0:D],
                                        xT[t.half][:].bitcast(F32).rearrange("p c t -> p (c t)"), ALU.subtract).then_inc(sem("xT_low"), 1)

            def on_low(t):
                ready(dve, "onT", t)
                freed(dve, "attn_ps", t)
                nc.vector.tensor_tensor(onT_low[t.half][:].rearrange("p c t -> p (c t)"), XT[:, 0:D],
                                        onT[t.half][:].bitcast(F32).rearrange("p c t -> p (c t)"), ALU.subtract).then_inc(sem("onT_low"), 1)

            def ln1_stats(t):
                landed(dve, "x_in", t)
                nc.vector.bn_stats(st1[t.half][:], xin[t.half][:]).then_inc(sem("ln1_st"), 1)

            def ln1_mean(t):
                freed(dve, "ln1_rs", t)
                ready(dve, "ln1_st", t)
                settle(dve)
                nc.vector.bn_aggr(mv1[t.half][:], st1[t.half][:]).then_inc(sem("ln1_mv"), 1)

            def ln1_rows(t):
                freed(dve, "xT_ps", t)
                scale_rows(t, xin[t.half][:], xn[t.half][:], mv1, rs1, "ln1", "ln1")

            def gate(t):
                ready(dve, "o_turned", t)
                ready(dve, "tg", t)
                freed(dve, "on", t)
                nc.vector.scalar_tensor_tensor(out=og[t.half][:], in0=tg[t.half][:], scalar=1.0,
                                               in1=M[:, 0:D], op0=ALU.add, op1=ALU.mult).then_inc(sem("og"), 1)

            def apply_decay(g):
                def part(t):
                    dve.wait_ge(sem("scored"), t.index() * 4 + g + 1)
                    freed(dve, "pv", t, back=1, per=4, at=g + 1)
                    if t.known() and t.index() == 0:
                        dve.wait_ge(sem("decay"), 1)
                    nc.vector.tensor_tensor(probs[:, 4 * g:4 * g + 4, :].rearrange("p h c -> p (h c)"), SC[g % 2][:, :],
                                            decay[:, 4 * g:4 * g + 4, :].rearrange("p h c -> p (h c)"), ALU.mult).then_inc(sem("probs"), 1)
                return part

            def state_out(t):
                if t.half == 0:
                    dve.wait_ge(sem("state_ps"), t.pair + 1)
                    if not (t.known() and t.index() == 0):
                        dve.wait_ge(sem("pv"), t.pair * 8)
                    nc.vector.tensor_tensor(state[:], OT[:, D:2 * D].rearrange("p (c e) -> p c e", c=KC),
                                            same_head[:].rearrange("p (a e) -> p a e", a=1).broadcast_to([P, KC, P]),
                                            ALU.mult).then_inc(sem("state"), 1)

            def head_sums(t):
                p = t.half
                ready(dve, "sq", t)
                nc.vector.tensor_reduce(hsum[p][:], sq[p][:].rearrange("p (h d) -> p h d", d=HD), AX.X,
                                        ALU.add).then_inc(sem("hsum"), 1)

            def head_mean(t):
                p = t.half
                ready(dve, "hsum", t)
                nc.vector.tensor_scalar(hmean[p][:], hsum[p][:], 1.0 / HD, 4 * EPS, ALU.mult, ALU.add).then_inc(sem("hmean"), 1)

            def half_bits(t):
                p = t.half
                ready(dve, "hmean", t)
                nc.vector.tensor_scalar(hbits[p][:], hmean[p][:].bitcast(U32), 1, None, ALU.logical_shift_right).then_inc(sem("hbits"), 1)

            def guess(t):
                p = t.half
                ready(dve, "hbits", t)
                nc.vector.tensor_scalar(hguess[p][:], hbits[p][:], -1.0, float(0x5F3759DF), ALU.mult, ALU.add).then_inc(sem("hguess"), 1)

            def square_root1(t):
                p = t.half
                ready(dve, "hguess", t)
                y = hguess[p][:].bitcast(F32)
                nc.vector.tensor_tensor(hsq[p][:], y, y, ALU.mult).then_inc(sem("hsq1"), 1)

            def times_mean1(t):
                p = t.half
                ready(dve, "hsq1", t)
                nc.vector.scalar_tensor_tensor(out=hstep[p][:], in0=hsq[p][:], scalar=-0.5, in1=hmean[p][:],
                                               op0=ALU.mult, op1=ALU.mult).then_inc(sem("hstep1"), 1)

            def root1(t):
                p = t.half
                ready(dve, "hstep1", t)
                nc.vector.scalar_tensor_tensor(out=hfirst[p][:], in0=hstep[p][:], scalar=1.5, in1=hguess[p][:].bitcast(F32),
                                               op0=ALU.add, op1=ALU.mult).then_inc(sem("hfirst"), 1)

            def square_root2(t):
                p = t.half
                ready(dve, "hfirst", t)
                nc.vector.tensor_tensor(hsq[p][:], hfirst[p][:], hfirst[p][:], ALU.mult).then_inc(sem("hsq2"), 1)

            def times_mean2(t):
                p = t.half
                ready(dve, "hsq2", t)
                nc.vector.tensor_tensor(hstep[p][:], hsq[p][:], hmean[p][:], ALU.mult).then_inc(sem("hstep2"), 1)

            def polynomial(t):
                p = t.half
                ready(dve, "hstep2", t)
                nc.vector.scalar_tensor_tensor(out=hpoly[p][:], in0=hstep[p][:], scalar=-10.0 / 3.0, in1=hstep[p][:],
                                               op0=ALU.add, op1=ALU.mult).then_inc(sem("hpoly"), 1)

            def root2(t):
                p = t.half
                ready(dve, "hpoly", t)
                freed(dve, "on", t)
                nc.vector.scalar_tensor_tensor(out=hroot[p][:], in0=hpoly[p][:], scalar=5.0, in1=hfirst[p][:],
                                               op0=ALU.add, op1=ALU.mult).then_inc(sem("hroot"), 1)

            def residual(t):
                ready(dve, "attn_ps", t)
                landed(dve, "res_in", t)
                res = pay[t.half][:, D:2 * D]
                nc.vector.tensor_tensor(res, res, M[:, D:2 * D], ALU.add).then_inc(sem("x1"), 1)

            def ln2_stats(t):
                ready(dve, "x1", t)
                nc.vector.bn_stats(st2[t.half][:], pay[t.half][:, D:2 * D]).then_inc(sem("ln2_st"), 1)

            def ln2_mean(t):
                freed(dve, "ln2_rs", t)
                ready(dve, "ln2_st", t)
                settle(dve)
                nc.vector.bn_aggr(mv2[t.half][:], st2[t.half][:]).then_inc(sem("ln2_mv"), 1)

            def ln2_rows(t):
                scale_rows(t, pay[t.half][:, D:2 * D], pay[t.half][:, 0:D], mv2, rs2, "ln2", "x2n")

            def probability(t):
                if t.known() and t.index() == 0:
                    dve.wait_ge(sem("ones"), 5)
                ready(dve, "th", t)
                nc.vector.tensor_scalar(route[t.half][:], th[t.half][:], 0.5, 0.5, ALU.mult, ALU.add).then_inc(sem("route"), 1)

            def best_of(t):
                ready(dve, "route", t)
                nc.vector.tensor_reduce(pay[t.half][:, ROW - 2:ROW - 1], route[t.half][:], AX.X, ALU.max).then_inc(sem("best"), 1)

            def candidates(t):
                p = t.half
                ready(dve, "best", t)
                nc.vector.scalar_tensor_tensor(out=cand[p][:], in0=route[p][:], scalar=pay[p][:, ROW - 2:ROW - 1], in1=desc[:],
                                               op0=ALU.is_equal, op1=ALU.mult).then_inc(sem("cand"), 1)

            def first_of(t):
                ready(dve, "cand", t)
                nc.vector.tensor_reduce(cmax[t.half][:], cand[t.half][:], AX.X, ALU.max).then_inc(sem("cmax"), 1)

            def chosen(t):
                ready(dve, "cmax", t)
                freed(dve, "rank_ps", t)
                nc.vector.tensor_scalar(mask[t.half][:], cand[t.half][:], cmax[t.half][:, 0:1], None, ALU.is_equal).then_inc(sem("mask"), 1)

            def rank_row(t):
                ready(dve, "rank_ps", t)
                nc.vector.tensor_tensor(rank[t.half][:], M[:, 16:16 + E], base[:], ALU.add).then_inc(sem("rank"), 1)

            def count(t):
                ready(dve, "rank_ps", t)
                nc.vector.tensor_tensor(seen[:], seen[:], mask[t.half][:], ALU.add).then_inc(sem("seen"), 1)

            def own_row(t):
                ready(dve, "rank", t)
                nc.vector.tensor_tensor(prod[t.half][:], rank[t.half][:], mask[t.half][:], ALU.mult).then_inc(sem("prod"), 1)

            def row_sum(t):
                ready(dve, "prod", t)
                nc.vector.tensor_reduce(posf[t.half][:], prod[t.half][:], AX.X, ALU.add).then_inc(sem("posf"), 1)

            def row_number(t):
                p = t.half
                ready(dve, "posf", t)
                if not (t.known() and t.index() < 2):
                    dve.wait_ge(sem(f"sorted{p}"), t.pair * 16)
                nc.vector.tensor_copy(pos[p][:], posf[p][:]).then_inc(sem("pos"), 1)

            def weights(t):
                if t.known() and t.index() == 0:
                    split_weights()
                if t.known() and t.index() == 1:
                    split_more_weights()
                    dve.wait_ge(sem("sh"), 3)
                    for a in range(2):
                        nc.vector.tensor_reduce(parity[:, a:a + 1], same_head[:, HD * a:P:2 * HD], AX.X, ALU.add).then_inc(sem("parity"), 1)

            dve.wait_ge(sem("ld_in"), 16)
            dve.wait_ge(sem("dist"), 4)
            nc.vector.tensor_tensor(decay[:], dist[:].rearrange("p (h c) -> p h c", h=1).broadcast_to([P, H, P]),
                                    ld_row[:].rearrange("p (h a) -> p h a", a=1).broadcast_to([P, H, P]),
                                    ALU.mult).then_inc(sem("decay_log"), 1)
            pipeline(dve, [(x_low, 1), (gate, -1), (apply_decay(0), 0), (ln2_rows, -2), (ln1_stats, 2),
                           (head_sums, -1), (ln1_mean, 2), (head_mean, -1), (half_bits, -1), (guess, -1),
                           (square_root1, -1), (ln1_rows, 2), (apply_decay(1), 0), (times_mean1, -1), (root1, -1),
                           (probability, -2), (square_root2, -1), (best_of, -2), (times_mean2, -1), (state_out, 0),
                           (candidates, -2), (polynomial, -1), (root2, -1), (first_of, -2), (apply_decay(2), 0),
                           (chosen, -2), (apply_decay(3), 0), (weights, 2), (rank_row, -2), (own_row, -2),
                           (on_low, -1), (row_sum, -2), (row_number, -2), (residual, -1), (count, -2),
                           (ln2_stats, -1), (ln2_mean, -1)])

            links = [0]

            def link(ins):
                links[0] += 1
                ins.then_inc(sem("table_step"), 1)
                dve.wait_ge(sem("table_step"), links[0])

            dve.wait_ge(sem("counts_ps"), 1)
            dve.wait_ge(sem("consts"), 6)
            link(nc.vector.tensor_copy(cnt[:], M[0:1, 32:32 + E]))
            link(nc.vector.tensor_tensor(fill_f[:], cnt[:], base[0:1, :], ALU.add))
            nc.vector.tensor_copy(fill_row[:], fill_f[:]).then_inc(sem("fill_row"), 1)
            link(nc.vector.tensor_tensor(over[:], cnt[:].rearrange("p (e a) -> p e a", a=1).broadcast_to([1, E, T]), steps[:], ALU.is_gt))
            link(nc.vector.tensor_reduce(need[:], over[:], AX.X, ALU.add))
            link(nc.vector.tensor_tensor_scan(last[:], need[:], zero_row[:], 0.0, ALU.add, ALU.add))

            def over_slots(row):
                return row.rearrange("p (a e) -> p a e", a=1).broadcast_to([1, SLOTS, E])

            link(nc.vector.tensor_tensor(t_behind[:], slot_no[:], over_slots(last[:]), ALU.is_ge))
            link(nc.vector.scalar_tensor_tensor(out=way[:], in0=need[:], scalar=-float(P), in1=way_e[:], op0=ALU.mult, op1=ALU.add))
            link(nc.vector.tensor_tensor(t_way[:], t_behind[:], over_slots(way[:]), ALU.mult))
            link(nc.vector.tensor_reduce(r_sum[:], t_way[:], AX.X, ALU.add))
            link(nc.vector.tensor_tensor(r_sum[:], r_sum[:], slot_start[:], ALU.add))
            nc.vector.tensor_scalar(slot_row[:], r_sum[:], float(E * ROOM), None, ALU.min).then_inc(sem("slot_row"), 1)
            link(nc.vector.tensor_reduce(w_sum[:], t_behind[:], AX.X, ALU.add))
            nc.vector.tensor_scalar(slot_w[:], w_sum[:], float(E - 1), float(EW), ALU.min, ALU.mult).then_inc(sem("slot_w"), 1)

            def hidden(s):
                ready(dve, "up_ps", s)
                ready(dve, "sg", s)
                freed(dve, "hT_ps", s)
                nc.vector.tensor_tensor(hh[s.half][:], sg[s.half][:], SC1[:, :], ALU.mult).then_inc(sem("hh"), 1)

            def combine(s):
                ready(dve, "down_ps", s)
                landed(dve, "rest_in", s)
                if not (s.known() and s.index() < 2):
                    dve.wait_ge(sem(f"stored{s.half}"), s.pair * 16)
                nc.vector.tensor_copy(tok_u[s.half][:], rest[s.half][:, D + 1:D + 2].bitcast(U32)).then_inc(sem("tok_u"), 1)
                ready(dve, "tok_u", s)
                nc.vector.scalar_tensor_tensor(out=yo[s.half][:], in0=M[:, 0:D], scalar=rest[s.half][:, D:D + 1],
                                               in1=rest[s.half][:, 0:D], op0=ALU.mult, op1=ALU.add).then_inc(sem("yo"), 1)

            expert_pipeline(dve, [(hidden, 0), (combine, -1)])

        @block.tensor
        def _(pe):
            pe.wait_ge(sem("ident"), 1)
            pe.wait_ge(sem("ld_exp"), 1)
            for c in range(KC):
                nc.tensor.transpose(TR[:, c * P:(c + 1) * P], ld_exp[:, c * P:(c + 1) * P], ident[:]).then_inc(sem("ld_T"), 1)
            pe.wait_ge(sem("w_g12_in"), 32)
            for c in range(KC):
                ins = nc.tensor.matmul(M[:, c * D:(c + 1) * D], w_g1T[:, c * P:(c + 1) * P], w_g2[:, :], start=True, stop=True)
            ins.then_inc(sem("w_g_ps"), 1)

            def three_passes(dst, high, low, w_high, w_low, low_ready):
                for c in range(KC):
                    nc.tensor.matmul(dst, high[:, c, :], w_high[:, c, :], start=(c == 0), stop=False)
                for c in range(KC):
                    nc.tensor.matmul(dst, high[:, c, :], w_low[:, c, :], start=False, stop=False)
                low_ready()
                for c in range(KC):
                    ins = nc.tensor.matmul(dst, low[:, c, :], w_high[:, c, :], start=False, stop=(c == KC - 1))
                return ins

            def x_turn(t):
                ready(pe, "ln1", t)
                freed(pe, "onT_low", t, back=3)
                for c in range(KC):
                    ins = nc.tensor.transpose(XT[:, c * P:(c + 1) * P], xn[t.half][:, c * P:(c + 1) * P], ident[:])
                ins.then_inc(sem("xT_ps"), 1)

            def qk_proj(t):
                ready(pe, "xT", t)
                freed(pe, "qk_silu", t, back=1)
                if t.known() and t.index() == 0:
                    pe.wait_ge(sem("w_qk"), 2)
                three_passes(PJ0[:, :], xT[t.half], xT_low[t.half], w_qkvg[:, :, 0:2 * D], w_qkvg_low[:, :, 0:2 * D],
                             lambda: ready(pe, "xT_low", t)).then_inc(sem("qk_ps"), 1)

            def vg_proj(t):
                freed(pe, "tg", t, back=1)
                if t.known() and t.index() == 0:
                    pe.wait_ge(sem("w_v"), 2)
                    pe.wait_ge(sem("w_g"), 2)
                three_passes(PJ1[:, :], xT[t.half], xT_low[t.half], w_qkvg[:, :, 2 * D:4 * D], w_qkvg_low[:, :, 2 * D:4 * D],
                             lambda: None).then_inc(sem("vg_ps"), 1)

            def qk_turn(t):
                ready(pe, "qk_silu", t)
                freed(pe, "qkT", t, back=1)
                if t.known() and t.index() == 0:
                    pe.wait_ge(sem("ld_col"), KC)
                for c in range(2 * KC):
                    ins = nc.tensor.transpose(TR[:, c * P:(c + 1) * P], qk[t.half][:, c * P:(c + 1) * P], ident[:])
                ins.then_inc(sem("qkT_ps"), 1)

            def score(g):
                def part(t):
                    if g == 0:
                        ready(pe, "qkT", t)
                    freed(pe, "probs", t, back=1, per=4, at=g + 3)
                    c, h = g // 2, 4 * (g % 2)
                    nc.tensor.matmul(SC[g % 2][:, :], qkT[t.half][:, KC + c, :],
                                     q_blocks[t.half][:, c, h:h + 4, :].rearrange("p h c -> p (h c)"),
                                     start=True, stop=True).then_inc(sem("scored"), 1)
                return part

            def state_product(t):
                if t.half == 0:
                    pe.wait_ge(sem("kd"), t.pair + 1)
                    ready(pe, "v", t, KC)
                    freed(pe, "oT", t, back=1)
                    for c in range(KC):
                        ins = nc.tensor.matmul(OT[:, D + c * P:D + (c + 1) * P], kd[:, c * P:(c + 1) * P], v_heads(vx[0], c),
                                               start=True, stop=True)
                    ins.then_inc(sem("state_ps"), 1)

            def pv(g):
                def part(t):
                    c = g // 2
                    if g == 0:
                        ready(pe, "v", t, KC)
                        freed(pe, "oT", t, back=1)
                        pe.wait_ge(sem("state"), t.pair + 1)
                        if t.half == 1:
                            pe.wait_ge(sem("qd"), t.pair + 1)
                    if t.half == 1 and g % 2 == 0:
                        nc.tensor.matmul(OT[:, c * P:(c + 1) * P], state[:, c, :], qd[:, c, :], start=True, stop=False,
                                         skip_group_check=True)
                    pe.wait_ge(sem("probs"), t.index() * 4 + g + 1)
                    for a in range(2):
                        for j in (2 * (g % 2), 2 * (g % 2) + 1):
                            head = c * HPC + 2 * j + a
                            ins = nc.tensor.matmul(OT[32 * j:32 * j + 32, c * P:(c + 1) * P], vx[t.half][:, c * HPC // 2 + j, a, :],
                                                   probs[:, head, :], start=(a == 0 and t.half == 0), stop=(a == 1),
                                                   skip_group_check=True)
                    ins.then_inc(sem("pv"), 1)
                return part

            def o_turn(t):
                ready(pe, "oT", t)
                freed(pe, "x1", t, back=1)
                for c in range(KC):
                    ins = nc.tensor.transpose(M[:, c * P:(c + 1) * P], oT[t.half][:, c, :], ident[:])
                ins.then_inc(sem("o_turned"), 1)

            def on_turn(t):
                ready(pe, "on", t)
                freed(pe, "x2T", t, back=1)
                ready(pe, "xT_low", t.later(2)) if not (t.known() and t.index() >= T - 2) else None
                for c in range(KC):
                    ins = nc.tensor.transpose(XT[:, c * P:(c + 1) * P], on[t.half][:, c * P:(c + 1) * P], ident[:])
                ins.then_inc(sem("on_turned"), 1)

            def attn_out(t):
                ready(pe, "onT", t)
                freed(pe, "rank", t, back=1)
                if t.known() and t.index() == 0:
                    pe.wait_ge(sem("w_o"), 3)
                three_passes(M[:, D:2 * D], onT[t.half], onT_low[t.half], w_o, w_o_low,
                             lambda: ready(pe, "onT_low", t)).then_inc(sem("attn_ps"), 1)

            def x2_turn(t):
                ready(pe, "x2n", t)
                if not (t.known() and t.index() >= T - 3):
                    ready(pe, "xT_low", t.later(3))
                else:
                    ready(pe, "onT_low", t)
                for c in range(KC):
                    ins = nc.tensor.transpose(XT[:, D + c * P:D + (c + 1) * P], pay[t.half][:, c * P:(c + 1) * P], ident[:])
                ins.then_inc(sem("x2T_ps"), 1)

            def logits(t):
                ready(pe, "x2T", t)
                if not (t.known() and t.index() == T - 1):
                    ready(pe, "og", t.later(1))
                if t.known() and t.index() == 0:
                    pe.wait_ge(sem("w_r_in"), 16)
                for c in range(KC):
                    ins = nc.tensor.matmul(M[:, 0:E], x2T[t.half][:, c, :], w_r[:, c, :], start=(c == 0), stop=(c == KC - 1))
                ins.then_inc(sem("logits_ps"), 1)

            def ranks(t):
                ready(pe, "mask", t)
                freed(pe, "seen", t, back=1)
                nc.tensor.matmul(M[:, 16:16 + E], upper[:], mask[t.half][:], start=True, stop=False)
                nc.tensor.matmul(M[:, 16:16 + E], ones_bf[:], seen[:], start=False, stop=True).then_inc(sem("rank_ps"), 1)

            pipeline(pe, [(x_turn, 1), (score(0), 0), (o_turn, -1), (qk_proj, 1), (score(1), 0), (x2_turn, -2),
                           (score(2), 0), (logits, -2), (qk_turn, 1), (state_product, 0), (vg_proj, 1),
                           (score(3), 0), (pv(0), 0), (on_turn, -1), (ranks, -2), (pv(1), 0), (pv(2), 0), (pv(3), 0),
                           (attn_out, -1)])

            pe.wait_ge(sem("seen"), T)
            pe.wait_ge(sem("rank"), T)
            nc.tensor.matmul(M[0:1, 32:32 + E], ones_bf[:, 0:1], seen[:], start=True, stop=True).then_inc(sem("counts_ps"), 1)

            pe.wait_ge(sem("w_exp"), 16 * 3 * E)
            pe.wait_ge(sem("slot_w"), 1)

            def weights_of(s):
                settle(pe)
                return nc.tensor.value_load(slot_w[0:1, bass.ds(s.index(), 1)], min_val=0, max_val=(E - 1) * EW)

            def xs_turn(s):
                landed(pe, "xs_in", s)
                freed(pe, "xsT", s, back=1)
                for c in range(KC):
                    ins = nc.tensor.transpose(XT[:, c * P:(c + 1) * P], xs[s.half][:, c * P:(c + 1) * P], ident[:])
                ins.then_inc(sem("xsT_ps"), 1)

            def gate2(s):
                ready(pe, "xsT", s)
                freed(pe, "sg", s, back=1)
                w = weights_of(s)
                for c in range(KC):
                    ins = nc.tensor.matmul(SC0[:, :], xsT[s.half][:, c, :], w_exp[:, bass.ds(w + c * F, F)],
                                           start=(c == 0), stop=(c == KC - 1))
                ins.then_inc(sem("gate2_ps"), 1)

            def up2(s):
                freed(pe, "hh", s, back=1)
                w = weights_of(s)
                for c in range(KC):
                    ins = nc.tensor.matmul(SC1[:, :], xsT[s.half][:, c, :], w_exp[:, bass.ds(w + (KC + c) * F, F)],
                                           start=(c == 0), stop=(c == KC - 1))
                ins.then_inc(sem("up_ps"), 1)

            def h_turn(s):
                ready(pe, "hh", s)
                freed(pe, "hT", s, back=1)
                for c in range(FC):
                    ins = nc.tensor.transpose(TR[:, c * P:(c + 1) * P], hh[s.half][:, c * P:(c + 1) * P], ident[:])
                ins.then_inc(sem("hT_ps"), 1)

            def down(s):
                ready(pe, "hT", s)
                freed(pe, "yo", s, back=1)
                w = weights_of(s)
                for c in range(FC):
                    ins = nc.tensor.matmul(M[:, 0:D], hT[s.half][:, c, :], w_exp[:, bass.ds(w + GU + c * D, D)],
                                           start=(c == 0), stop=(c == FC - 1))
                ins.then_inc(sem("down_ps"), 1)

            expert_pipeline(pe, [(gate2, 0), (h_turn, -1), (up2, 0), (xs_turn, 1), (down, -1)])


_INS = ["L0_attn_x", "L0_attn_log_decay", "L0_attn_Wq", "L0_attn_Wk", "L0_attn_Wv", "L0_attn_Wo", "L0_attn_Wg1",
        "L0_attn_Wg2", "L0_attn_norm_w", "L0_ffn_router_w", "L0_ffn_gate_w", "L0_ffn_up_w", "L0_ffn_down_w"]


def kernel(**inputs):
    import numpy as np
    import concourse.bacc as bacc
    from concourse.bass_utils import run_bass_kernel_spmd

    nc = bacc.Bacc("TRN2", target_bir_lowering=False, num_devices=1)
    arrays, args = {}, []
    for name in _INS:
        a = np.ascontiguousarray(inputs[name])
        arrays[f"in_{name}"] = a
        args.append(nc.dram_tensor(f"in_{name}", a.shape, mybir.dt.from_np(a.dtype), kind="ExternalInput").ap())
    out = nc.dram_tensor("out", inputs["L0_attn_x"].shape, F32, kind="ExternalOutput").ap()
    lightning_block(nc, *args, out)
    r = run_bass_kernel_spmd(nc, [arrays], core_ids=[0])
    return r.results[0]["out"]
```
